# Optimizing a Trainium2 kernel written in Bass

```python
import numpy as np
import jax
import jax.numpy as jnp

def _softmax(x, axis=-1):
    return jax.nn.softmax(x, axis=axis)

def _gelu(x):
    return jax.nn.gelu(x, approximate=True)

def _silu(x):
    return jax.nn.silu(x)

def _sigmoid(x):
    return jax.nn.sigmoid(x)

def _layernorm(x, axis=-1, eps=1e-05):
    m = jnp.mean(x, axis=axis, keepdims=True)
    v = jnp.var(x, axis=axis, keepdims=True)
    return (x - m) / jnp.sqrt(v + eps)

def _scatter_add(tgt, idx, src, axis=0):
    return tgt.at[idx].add(src)

def _segment_sum(src, seg, n):
    return jax.ops.segment_sum(src, seg, n)
kernel_name = 'mk_cond_resid_d2_seqx_r8_217b00'

def setup_inputs(seed: int=0):
    np.random.seed(seed)
    _w = jnp.asarray

    def _rec_inputs():
        import jax
        import jax.numpy as jnp
        _rk = jax.random.key(seed)
        x = -0.0005207 + 1.001 * jax.random.normal(jax.random.fold_in(_rk, 1), (32, 32, 512), jnp.float32)
        _lenS = 32 - jax.random.randint(jax.random.fold_in(_rk, 7), (32,), 0, max(1, 32 // 4) + 1, jnp.int32)
        _lenS2 = 32 - jax.random.randint(jax.random.fold_in(_rk, 8), (32,), 0, max(1, 32 // 4) + 1, jnp.int32)
        itok_Bx16_0_63 = jax.random.randint(jax.random.fold_in(_rk, 11), (32, 16), 0, 64, jnp.int32)
        itok_B_207_1644 = jax.random.randint(jax.random.fold_in(_rk, 12), (32,), 207, 1645, jnp.int32)
        itok_B_0_15 = jax.random.randint(jax.random.fold_in(_rk, 13), (32,), 0, 16, jnp.int32)
        return (x, itok_Bx16_0_63, itok_B_207_1644, itok_B_0_15)
    x, itok_Bx16_0_63, itok_B_207_1644, itok_B_0_15 = _rec_inputs()

    def _L0_cond_setup():
        import jax, jax.numpy as jnp
        import numpy as np
        B, S, HID = (4, 128, 512)
        D, HQ, HK = (128, 32, 8)
        PAGES, PSIZE, NPP = (64, 32, 16)
        THETA = 10000.0
        EPS = 1e-06
        SCALE = 1.0 / float(np.sqrt(D))

        def _rmsnorm(t, w):
            var = jnp.mean(t * t, axis=-1, keepdims=True)
            return t * jax.lax.rsqrt(var + EPS) * w

        def _rope(t, pos):
            inv_freq = 1.0 / THETA ** (jnp.arange(0, D, 2, dtype=jnp.float32) / D)
            freqs = pos[..., None].astype(jnp.float32) * inv_freq
            cos = jnp.cos(freqs)[:, :, None, :]
            sin = jnp.sin(freqs)[:, :, None, :]
            t1, t2 = (t[..., :D // 2], t[..., D // 2:])
            return jnp.concatenate([t1 * cos - t2 * sin, t2 * cos + t1 * sin], axis=-1)
        key = jax.random.key(seed)
        ks = jax.random.split(key, 10)
        x = jax.random.normal(ks[0], (B, S, HID), jnp.float32)
        Wq = jax.random.normal(ks[1], (HQ * D, HID), jnp.float32) * 0.02
        Wk = jax.random.normal(ks[2], (HK * D, HID), jnp.float32) * 0.02
        Wv = jax.random.normal(ks[3], (HK * D, HID), jnp.float32) * 0.02
        Wo = jax.random.normal(ks[4], (HID, HQ * D), jnp.float32) * 0.02
        q_norm_w = jax.random.uniform(ks[5], (D,), jnp.float32)
        k_norm_w = jax.random.uniform(ks[6], (D,), jnp.float32)
        k_cache = jax.random.normal(ks[7], (PAGES, PSIZE, HK, D), jnp.float32)
        v_cache = jax.random.normal(ks[8], (PAGES, PSIZE, HK, D), jnp.float32)
        block_table = jnp.arange(B * NPP, dtype=jnp.int32).reshape(B, NPP)
        cache_seqlens = jax.random.randint(ks[9], (B,), 0, 475).astype(jnp.int32)
        return dict(x=x, Wq=Wq, Wk=Wk, Wv=Wv, Wo=Wo, q_norm_w=q_norm_w, k_norm_w=k_norm_w, k_cache=k_cache, v_cache=v_cache, block_table=block_table, cache_seqlens=cache_seqlens)
    _L0_cond_all = _L0_cond_setup()
    _L0_cond_in = {k: v for k, v in _L0_cond_all.items() if k in ('Wq', 'Wk', 'Wv', 'Wo', 'q_norm_w', 'k_norm_w', 'k_cache', 'v_cache')}
    del _L0_cond_all

    def _L1_cond_setup():
        import jax, jax.numpy as jnp
        import numpy as np
        B, C, T = (64, 32, 512)
        S, D = (16, 32)
        key = jax.random.key(seed)
        k1, k2, k3 = jax.random.split(key, 3)
        x = jax.random.normal(k1, (B, C, T), dtype=jnp.float32)
        condition = jax.random.randint(k2, (B,), 0, S, dtype=jnp.int64)
        bound = float(np.sqrt(6.0 / C))
        weights = jax.random.uniform(k3, (S, C, D), dtype=jnp.float32, minval=-bound, maxval=bound)
        return {'x': x, 'condition': condition, 'weights': weights}
    _L1_cond_all = _L1_cond_setup()
    _L1_cond_in = {k: v for k, v in _L1_cond_all.items() if k in ('weights',)}
    del _L1_cond_all
    return {'x': x, 'itok_Bx16_0_63': itok_Bx16_0_63, 'itok_B_207_1644': itok_B_207_1644, 'itok_B_0_15': itok_B_0_15, 'L0_cond_Wq': _L0_cond_in['Wq'], 'L0_cond_Wk': _L0_cond_in['Wk'], 'L0_cond_Wv': _L0_cond_in['Wv'], 'L0_cond_Wo': _L0_cond_in['Wo'], 'L0_cond_q_norm_w': _L0_cond_in['q_norm_w'], 'L0_cond_k_norm_w': _L0_cond_in['k_norm_w'], 'L0_cond_k_cache': _L0_cond_in['k_cache'], 'L0_cond_v_cache': _L0_cond_in['v_cache'], 'L1_cond_weights': _L1_cond_in['weights']}

def reference(x, itok_Bx16_0_63, itok_B_207_1644, itok_B_0_15, L0_cond_Wq, L0_cond_Wk, L0_cond_Wv, L0_cond_Wo, L0_cond_q_norm_w, L0_cond_k_norm_w, L0_cond_k_cache, L0_cond_v_cache, L1_cond_weights):
    import jax
    import jax.numpy as jnp

    def _L0_cond_ref(x, Wq, Wk, Wv, Wo, q_norm_w, k_norm_w, k_cache, v_cache, block_table, cache_seqlens):
        import jax, jax.numpy as jnp
        import numpy as np
        B, S, HID = (4, 128, 512)
        D, HQ, HK = (128, 32, 8)
        PAGES, PSIZE, NPP = (64, 32, 16)
        THETA = 10000.0
        EPS = 1e-06
        SCALE = 1.0 / float(np.sqrt(D))

        def _rmsnorm(t, w):
            var = jnp.mean(t * t, axis=-1, keepdims=True)
            return t * jax.lax.rsqrt(var + EPS) * w

        def _rope(t, pos):
            inv_freq = 1.0 / THETA ** (jnp.arange(0, D, 2, dtype=jnp.float32) / D)
            freqs = pos[..., None].astype(jnp.float32) * inv_freq
            cos = jnp.cos(freqs)[:, :, None, :]
            sin = jnp.sin(freqs)[:, :, None, :]
            t1, t2 = (t[..., :D // 2], t[..., D // 2:])
            return jnp.concatenate([t1 * cos - t2 * sin, t2 * cos + t1 * sin], axis=-1)
        bsz, seqlen, _ = x.shape
        q = jnp.einsum('bsd,ed->bse', x, Wq).reshape(bsz, seqlen, HQ, D)
        k = jnp.einsum('bsd,ed->bse', x, Wk).reshape(bsz, seqlen, HK, D)
        v = jnp.einsum('bsd,ed->bse', x, Wv).reshape(bsz, seqlen, HK, D)
        q = _rmsnorm(q, q_norm_w)
        k = _rmsnorm(k, k_norm_w)
        pos = cache_seqlens[:, None] + jnp.arange(seqlen)[None, :]
        q = _rope(q, pos)
        k = _rope(k, pos)
        L = NPP * PSIZE
        kc = k_cache[block_table].reshape(bsz, L, HK, D)
        vc = v_cache[block_table].reshape(bsz, L, HK, D)
        k_all = jnp.concatenate([kc, k], axis=1)
        v_all = jnp.concatenate([vc, v], axis=1)
        valid_c = jnp.arange(L)[None, :] < cache_seqlens[:, None]
        valid = jnp.concatenate([valid_c, jnp.ones((bsz, seqlen), dtype=bool)], axis=1)
        rep = HQ // HK
        k_all = jnp.repeat(k_all, rep, axis=2)
        v_all = jnp.repeat(v_all, rep, axis=2)
        scores = jnp.einsum('bqhd,bkhd->bhqk', q, k_all) * SCALE
        scores = jnp.where(valid[:, None, None, :], scores, -1e+30)
        probs = jax.nn.softmax(scores, axis=-1)
        o = jnp.einsum('bhqk,bkhd->bqhd', probs, v_all)
        o = o.reshape(bsz, seqlen, HQ * D)
        return jnp.einsum('bse,de->bsd', o, Wo)

    def _L1_cond_ref(x, condition, weights):
        import jax, jax.numpy as jnp
        import numpy as np
        B, C, T = (64, 32, 512)
        S, D = (16, 32)
        W = weights[condition]
        return jnp.einsum('bct,bcd->bdt', x, W)
    x = x + _L0_cond_ref(x, L0_cond_Wq, L0_cond_Wk, L0_cond_Wv, L0_cond_Wo, L0_cond_q_norm_w, L0_cond_k_norm_w, L0_cond_k_cache, L0_cond_v_cache, itok_Bx16_0_63, itok_B_207_1644)
    x = x + _L1_cond_ref(x, itok_B_0_15, L1_cond_weights)
    return x

_drawn_inputs = setup_inputs


def setup_inputs(seed=0):
    import zlib

    import numpy as np

    out = dict(_drawn_inputs(seed))
    spreads = {}
    factors = {'L0_cond_Wk': 8.0,
     'L0_cond_Wv': 8.0,
     'L0_cond_k_norm_w': 8.0,
     'L0_cond_k_cache': 4.297,
     'L0_cond_v_cache': 3.16}
    for name, (base, spread) in spreads.items():
        noise = np.random.default_rng([zlib.crc32(name.encode()), seed]).standard_normal(out[name].shape)
        drawn = base * np.exp(spread * noise) if base else spread * noise
        out[name] = jnp.asarray(drawn.astype(out[name].dtype))
    for name, factor in factors.items():
        out[name] = (out[name] * factor).astype(out[name].dtype)
    return out
```

```python
from contextlib import ExitStack

import numpy as np
import concourse.bass as bass
from concourse import mybir

F32 = mybir.dt.float32
F32R = mybir.dt.float32r
I32 = mybir.dt.int32
ALU = mybir.AluOpType
ACT = mybir.ActivationFunctionType
AX = mybir.AxisListType

P = 128
B, S, HID = 32, 32, 512
D, HQ, HK = 128, 32, 8
R = HQ // HK
PAGES, PSIZE, NPP = 64, 32, 16
CACHED = NPP * PSIZE
KEYS = CACHED + S
HALF = KEYS // 2
NPG = NPP + 1
TOK = B * S
TILES = TOK // P
BT = P // S
KC = HID // P
NC_ = 512
CHUNKS = 2 * HK * D // NC_ + HQ * D // NC_
EPS = 1e-6
SCALE = 1.0 / float(np.sqrt(D))
MASKED = -1e30
UNITS = B * HK
VCH = CACHED // P
TRIP = 16
MAGIC = 1.5 * 2.0 ** 23
PI2_A = 6.28125
PI2_B = float(np.float32(np.floor((2 * np.pi - PI2_A) * 2.0 ** 20) / 2.0 ** 20))
PI2_C = float(np.float32(2 * np.pi - PI2_A - PI2_B))


class Unit:

    def __init__(self, base, j):
        self.base, self.j = base, j

    def back(self, n):
        return Unit(self.base, self.j - n)

    def n(self, plus=0):
        return self.base + (self.j + plus)

    def static(self):
        return isinstance(self.base, int)

    def within(self, end):
        return not self.static() or 0 <= self.n() < end

    def slot(self, k):
        return self.j % k


def wait(eng, sem, value):
    if not isinstance(value, int) or value > 0:
        eng.wait_ge(sem, value)


def waits(eng, passed, pairs):
    for sem, v in pairs:
        wait(eng, sem, v)
    eng.sem_inc(passed, 1)


class Scope:
    def __init__(self, nc):
        self.nc, self.ctx = nc, ExitStack()

    def sb(self, name, shape, dt=F32):
        return self.ctx.enter_context(self.nc.sbuf_tensor(name, shape, dt))

    def ps(self, name, shape, dt=F32):
        return self.ctx.enter_context(self.nc.psum_tensor(name, shape, dt))

    def sem(self, name):
        return self.ctx.enter_context(self.nc.semaphore(name))


def heads4(ap):
    return ap.rearrange("p (h d) -> p h d", d=D)


def project(nc, top, xT, w_all, seq, inv_freq, sidx, q_w, k_w, kq_f, v_f, ident_d, ident, q_scale, q_nscale):
    s = Scope(nc)
    sb, sem = s.sb, s.sem
    with s.ctx:
        x_raw = sb("x_raw", [P, KC, TOK])
        x_hi = sb("x_hi", [P, KC, TOK], F32R)
        x_lo = sb("x_lo", [P, KC, TOK], F32R)
        w_raw = sb("w_raw", [P, 2, KC, NC_])
        w_hi = sb("w_hi", [P, 2, KC, NC_], F32R)
        w_lo = sb("w_lo", [P, 2, KC, NC_], F32R)
        pos_i = sb("pos_i", [P, TILES], I32)
        pos_f = sb("pos_f", [P, TILES])
        s_of_p = sb("s_of_p", [P, 1])
        inv = sb("inv", [P, D // 2])
        wb = sb("wb", [P, 2, D])
        ang = sb("ang", [P, TILES, D // 2])
        turn = sb("turn", [P, TILES, D // 2])
        sin_t = sb("sin_t", [P, TILES, D // 2])
        cos_t = sb("cos_t", [P, TILES, D // 2])
        rope_c = sb("rope_c", [P, 2, TILES, D])
        rope_s = sb("rope_s", [P, 2, TILES, D])
        sq = sb("sq", [P, 2, NC_])
        raw = sb("raw", [P, 2, NC_])
        m1 = sb("m1", [P, 2, NC_])
        m2 = sb("m2", [P, 2, NC_])
        rp = sb("rp", [P, 4, NC_])
        outb = sb("outb", [P, 4, NC_])
        ss = sb("ss", [P, 2, 4])
        ms = sb("ms", [P, 2, 4])
        k_rs = sb("k_rs", [P, 2, 4])
        q_rs = sb("q_rs", [P, TILES, HQ])
        minus_half = sb("minus_half", [P, 4])
        QP = [s.ps(f"QP{i}", [P, NC_]) for i in range(4)]
        TP = [s.ps(f"TP{i}", [P, NC_]) for i in range(4)]

        x_in, small_in, ident_in = sem("x_in"), sem("small_in"), sem("ident_in")
        w_in = [sem("w_in0"), sem("w_in1")]
        x_hi_done, x_split = sem("x_hi_done"), sem("x_split")
        w_hi_done, w_split = sem("w_hi_done"), sem("w_split")
        tab, trig = sem("tab"), sem("trig")
        mm_done, qp_read, m1_done = sem("mm_done"), sem("qp_read"), sem("m1_done")
        sq_done = sem("sq_done")
        ss_done, ms_done, rs_done = sem("ss_done"), sem("ms_done"), sem("rs_done")
        m2_done, add_done, rp_done = sem("m2_done"), sem("add_done"), sem("rp_done")
        t_done, t_evac = sem("t_done"), sem("t_evac")
        out_sent = [sem(f"out_sent{i}") for i in range(4)]
        const_set, table_step, scale_moved = sem("const_set"), sem("table_step"), sem("scale_moved")

        KU = 2 * TILES
        NU = CHUNKS * TILES

        def kind(u):
            if not u.static():
                return "q"
            return "v" if u.n() < KU else "k" if u.n() < 2 * KU else "q"

        def turned(u):
            return u.n(-KU)

        def run(eng, step, lag):
            pairs = NU // TRIP
            for pair in range(2):
                for j in range(TRIP):
                    step(Unit(pair * TRIP, j))
            with eng.Fori(2, pairs - 1) as pair:
                for j in range(TRIP):
                    step(Unit(pair * TRIP, j))
            for j in range(TRIP + lag):
                step(Unit((pairs - 1) * TRIP, j))

        block = s.ctx.enter_context(nc.Block())

        @block.sync
        def _(sp):
            sp.dma_start(x_raw[:, :, :], xT).then_inc(x_in, 16)
            sp.dma_start(w_raw[:, 0, :, :], w_all[0]).then_inc(w_in[0], 16)
            for bl in range(BT):
                src = seq[bl * TILES:(bl + 1) * TILES].partition_broadcast(S)
                sp.dma_start(pos_i[bl * S:(bl + 1) * S, :], src).then_inc(small_in, 16)
            sp.dma_start(s_of_p[:, :], sidx).then_inc(small_in, 16)
            sp.dma_start(inv[:, :], inv_freq.partition_broadcast(P)).then_inc(small_in, 16)
            sp.dma_start(wb[:, 0, :], q_w.partition_broadcast(P)).then_inc(small_in, 16)
            sp.dma_start(wb[:, 1, :], k_w.partition_broadcast(P)).then_inc(small_in, 16)
            sp.dma_start(ident[:, :], ident_d).then_inc(ident_in, 16)
            sp.dma_start(w_raw[:, 1, :, :], w_all[1]).then_inc(w_in[1], 16)

            def step(u):
                if u.slot(TILES) == 2 and (not u.static() or u.n() // TILES + 2 < CHUNKS):
                    chunk = Unit(u.base // TILES, u.j // TILES)
                    slot = (u.j // TILES) % 2
                    wait(sp, w_split, chunk.n(1))
                    sp.dma_start(w_raw[:, slot, :, :], w_all[bass.ds(chunk.n(2), 1)].rearrange("o p k n -> p (o k) n")).then_inc(w_in[slot], 16)
                v = u.back(2)
                if not v.within(NU):
                    return
                o = v.slot(4)
                wait(sp, t_evac, v.n(1))
                tile = v.j % TILES
                if kind(v) == "v":
                    chunk = v.n() // TILES
                    dst = v_f[tile * P:(tile + 1) * P, chunk * NC_:(chunk + 1) * NC_]
                    src = outb[:, o, :]
                else:
                    col = (v.base // TILES + (v.j // TILES - 2)) * P
                    dst = kq_f[tile * BT:(tile + 1) * BT, :, bass.ds(col, P)].rearrange("b d c -> d b c")
                    src = outb[:, o, :].rearrange("p (b c) -> p b c", b=BT)
                sp.dma_start(dst, src).then_inc(out_sent[o], 16)

            run(sp, step, 2)
            for o in range(4):
                sp.wait_ge(out_sent[o], 16 * NU // 4)

        @block.tensor
        def _(pe):
            pe.wait_ge(ident_in, 16)
            pe.wait_ge(x_split, 1)

            def step(u):
                if u.within(NU):
                    if u.slot(TILES) == 0:
                        wait(pe, w_split, (u.n() // TILES if u.static() else u.base // TILES + u.j // TILES) + 1)
                    wait(pe, qp_read, u.n(-3))
                    tile, slot = u.j % TILES, (u.j // TILES) % 2
                    cols = slice(tile * P, (tile + 1) * P)
                    bank = QP[u.slot(4)]
                    for k in range(KC):
                        nc.tensor.matmul(bank[:, :], x_hi[:, k, cols], w_hi[:, slot, k, :], start=(k == 0), stop=False)
                        nc.tensor.matmul(bank[:, :], x_hi[:, k, cols], w_lo[:, slot, k, :], start=False, stop=False)
                        mm = nc.tensor.matmul(bank[:, :], x_lo[:, k, cols], w_hi[:, slot, k, :], start=False, stop=(k == KC - 1))
                    mm.then_inc(mm_done, 1)
                v = u.back(2)
                if v.within(NU) and kind(v) != "v":
                    wait(pe, rp_done, turned(v) + 1)
                    wait(pe, t_evac, v.n(-3))
                    for h in range(4):
                        tr = nc.tensor.transpose(TP[v.slot(4)][:, h * P:(h + 1) * P], rp[:, v.slot(4), h * D:(h + 1) * D], ident[:, :])
                    tr.then_inc(t_done, 1)

            run(pe, step, 2)

        @block.scalar
        def _(act):
            act.wait_ge(tab, 1)
            nc.scalar.activation(sin_t[:, :, :], sin_t[:, :, :], ACT.Sin).then_inc(trig, 1)
            nc.scalar.activation(cos_t[:, :, :], cos_t[:, :, :], ACT.Sin).then_inc(trig, 1)

            def step(u):
                if u.within(NU):
                    bank = QP[u.slot(4)]
                    wait(act, mm_done, u.n(1))
                    if kind(u) == "v":
                        o = u.slot(4)
                        wait(act, out_sent[o], u.n(-o) * 4)
                        nc.scalar.copy(outb[:, o, :], bank[:, :]).then_inc(qp_read, 1)
                    else:
                        wait(act, ss_done, turned(u) - 1)
                        nc.scalar.activation(sq[:, u.slot(2), :], bank[:, :], ACT.Square).then_inc(sq_done, 1)
                        wait(act, m1_done, turned(u) - 1)
                        wait(act, m2_done, turned(u) - 1)
                        nc.scalar.copy(raw[:, u.slot(2), :], bank[:, :]).then_inc(qp_read, 1)
                v = u.back(2)
                if v.within(NU):
                    if kind(v) == "v":
                        wait(act, qp_read, v.n(1))
                        act.sem_inc(t_evac, 1)
                    else:
                        o = v.slot(4)
                        wait(act, t_done, turned(v) + 1)
                        wait(act, out_sent[o], v.n(-o) * 4)
                        dst = outb[:, o, :].rearrange("p (b r s) -> p r b s", b=BT, r=4)
                        src = TP[v.slot(4)][:, :].rearrange("p (r b s) -> p r b s", b=BT, r=4)
                        nc.scalar.copy(dst, src).then_inc(t_evac, 1)

            run(act, step, 2)

        @block.gpsimd
        def _(pool):
            nc.gpsimd.memset(minus_half[:, :], -0.5).then_inc(const_set, 1)
            pool.wait_ge(const_set, 1)

            def step(u):
                if kind(u) == "v":
                    return
                n, p2, qk = turned(u), u.slot(2), int(kind(u) == "k")
                tile = u.j % TILES
                wait(pool, qp_read, u.n(1))
                wait(pool, rp_done, n - 1)
                r, o = heads4(raw[:, p2, :]), heads4(m2[:, p2, :])
                for half in range(2):
                    a, c = half * 64, (1 - half) * 64
                    tt = nc.gpsimd.tensor_tensor(o[:, :, a:a + 64], r[:, :, c:c + 64],
                                                 rope_s[:, qk, tile:tile + 1, a:a + 64].to_broadcast([P, 4, 64]), ALU.mult)
                tt.then_inc(m2_done, 1)
                wait(pool, ms_done, n + 1)
                if qk:
                    rs = k_rs[:, p2, :]
                else:
                    rs = q_rs[:, tile, bass.ds((u.base // TILES + (u.j // TILES - 4)) * 4, 4)]
                nc.gpsimd.tensor_tensor(rs, ms[:, p2, :], minus_half[:, :], ALU.pow).then_inc(rs_done, 1)

            pool.wait_ge(tab, 2)
            run(pool, step, 0)

        @block.vector
        def _(dve):
            link = [0]

            def then(ins):
                link[0] += 1
                ins.then_inc(table_step, 1)
                dve.wait_ge(table_step, link[0])

            def split_w_piece(slot, k, part, chunk):
                if part == 0:
                    nc.vector.tensor_copy(w_hi[:, slot, k, :], w_raw[:, slot, k, :]).then_inc(w_hi_done, 1)
                else:
                    wait(dve, w_hi_done, chunk.n() * KC + (k + 1))
                    ins = nc.vector.tensor_tensor(w_lo[:, slot, k, :], w_raw[:, slot, k, :], w_hi[:, slot, k, :].bitcast(F32), ALU.subtract)
                    if k == KC - 1:
                        ins.then_inc(w_split, 1)

            dve.wait_ge(small_in, 16 * (BT + 4))
            then(nc.vector.tensor_copy(pos_f[:, :], pos_i[:, :]))
            then(nc.vector.tensor_scalar(pos_f[:, :], pos_f[:, :], s_of_p[:, :], None, ALU.add))
            then(nc.vector.tensor_tensor(ang[:, :, :], pos_f[:, :].unsqueeze(2).to_broadcast([P, TILES, D // 2]),
                                         inv[:, :].unsqueeze(1).to_broadcast([P, TILES, D // 2]), ALU.mult))
            for t, off in ((sin_t, 0.0), (cos_t, 0.25)):
                then(nc.vector.tensor_scalar(turn[:, :, :], ang[:, :, :], 1 / (2 * np.pi), off, ALU.mult, ALU.add))
                then(nc.vector.tensor_scalar(turn[:, :, :], turn[:, :, :], MAGIC, MAGIC, ALU.add, ALU.subtract))
                then(nc.vector.scalar_tensor_tensor(t[:, :, :], turn[:, :, :], -PI2_A, ang[:, :, :], ALU.mult, ALU.add))
                then(nc.vector.scalar_tensor_tensor(t[:, :, :], turn[:, :, :], -PI2_B, t[:, :, :], ALU.mult, ALU.add))
                then(nc.vector.scalar_tensor_tensor(t[:, :, :], turn[:, :, :], -PI2_C, t[:, :, :], ALU.mult, ALU.add))
                if off:
                    then(nc.vector.tensor_scalar(t[:, :, :], t[:, :, :], float(np.pi / 2), None, ALU.add))
                then(nc.vector.tensor_scalar(t[:, :, :], t[:, :, :], 3.1415925, -3.1415925, ALU.min, ALU.max))
            nc.vector.memset(ms[:, :, :], 0.0).then_inc(tab, 1)
            dve.wait_ge(x_in, 16)
            nc.vector.tensor_copy(x_hi[:, :, :], x_raw[:, :, :]).then_inc(x_hi_done, 1)
            dve.wait_ge(x_hi_done, 1)
            nc.vector.tensor_tensor(x_lo[:, :, :], x_raw[:, :, :], x_hi[:, :, :].bitcast(F32), ALU.subtract).then_inc(x_split, 1)
            dve.wait_ge(w_in[0], 16)
            for k in range(KC):
                for part in range(2):
                    split_w_piece(0, k, part, Unit(0, 0))
            dve.wait_ge(trig, 2)
            for qk in range(2):
                w1 = wb[:, qk:qk + 1, 0:64].to_broadcast([P, TILES, 64])
                w2 = wb[:, qk:qk + 1, 64:128].to_broadcast([P, TILES, 64])
                nc.vector.tensor_tensor(rope_c[:, qk, :, 0:64], cos_t[:, :, :], w1, ALU.mult)
                nc.vector.tensor_tensor(rope_c[:, qk, :, 64:128], cos_t[:, :, :], w2, ALU.mult)
                nc.vector.scalar_tensor_tensor(rope_s[:, qk, :, 0:64], sin_t[:, :, :], -1.0, w2, ALU.mult, ALU.mult)
                last = nc.vector.tensor_tensor(rope_s[:, qk, :, 64:128], sin_t[:, :, :], w1, ALU.mult)
            last.then_inc(tab, 1)
            dve.wait_ge(tab, 2)

            def step(u):
                p2, tile = u.slot(2), u.j % TILES
                if kind(u) != "v":
                    n, qk = turned(u), int(kind(u) == "k")
                    wait(dve, qp_read, u.n(1))
                    wait(dve, rp_done, n - 1)
                    nc.vector.tensor_tensor(heads4(m1[:, p2, :]), heads4(raw[:, p2, :]),
                                            rope_c[:, qk, tile:tile + 1, :].to_broadcast([P, 4, D]), ALU.mult).then_inc(m1_done, 1)
                nxt = Unit(u.base // TILES, u.j // TILES + 1)
                if not nxt.static() or nxt.n() < CHUNKS:
                    slot = (u.j // TILES + 1) % 2
                    if tile == 0:
                        wait(dve, w_in[slot], (nxt.base // 2 + (nxt.j // 2 + 1)) * 16)
                        wait(dve, mm_done, u.n())
                    split_w_piece(slot, tile // 2, tile % 2, nxt)
                if kind(u) == "v":
                    return
                wait(dve, sq_done, n + 1)
                wait(dve, rs_done, n - 1)
                nc.vector.reduce_sum(ss[:, p2, :], heads4(sq[:, p2, :]), AX.X).then_inc(ss_done, 1)
                wait(dve, ss_done, n + 1)
                nc.vector.tensor_scalar(ms[:, p2, :], ss[:, p2, :], 1.0 / D, EPS, ALU.mult, ALU.add).then_inc(ms_done, 1)
                wait(dve, m2_done, n + 1)
                wait(dve, m1_done, n + 1)
                wait(dve, t_done, n - 3)
                if qk:
                    nc.vector.tensor_tensor(m1[:, p2, :], m1[:, p2, :], m2[:, p2, :], ALU.add).then_inc(add_done, 1)
                    wait(dve, add_done, n + 1)
                    wait(dve, rs_done, n + 1)
                    nc.vector.tensor_tensor(heads4(rp[:, u.slot(4), :]), heads4(m1[:, p2, :]),
                                            k_rs[:, p2, :].unsqueeze(2).to_broadcast([P, 4, D]), ALU.mult).then_inc(rp_done, 1)
                else:
                    nc.vector.tensor_tensor(rp[:, u.slot(4), :], m1[:, p2, :], m2[:, p2, :], ALU.add).then_inc(rp_done, 1)

            run(dve, step, 0)
            dve.wait_ge(rs_done, (CHUNKS - 2) * TILES)
            qs = q_scale[:, :].rearrange("p (t b k) -> p t b k", b=BT, k=HK)
            qr = q_rs[:, :, :].rearrange("p t (k r) -> p t k r", r=R)
            for bl in range(BT):
                for r in range(R):
                    last = nc.vector.tensor_scalar(qs[r * S:(r + 1) * S, :, bl, :], qr[bl * S:(bl + 1) * S, :, :, r], SCALE, None, ALU.mult)
            last.then_inc(scale_moved, 1)
            dve.wait_ge(scale_moved, 1)
            nc.vector.tensor_scalar(q_nscale[:, :], q_scale[:, :], -1.0, None, ALU.mult)


def attend(nc, seq, pages, page_of_chunk, sidx, kT, v_c, iota, kq_f, v_f, o_f, ident, q_scale, q_nscale):
    s = Scope(nc)
    sb, sem = s.sb, s.sem
    with s.ctx:
        NS = 4
        CONST = 16 * (4 + BT)
        k_raw = sb("k_raw", [P, 2, NPG, HK * PSIZE])
        v_raw = sb("v_raw", [P, 2, VCH, HK * D])
        v_fresh = sb("v_fresh", [S, 2, HK * D])
        q_raw = sb("q_raw", [P, 2, HK * P])
        k_hi = sb("k_hi", [P, NS, KEYS], F32R)
        k_lo = sb("k_lo", [P, NS, KEYS], F32R)
        q_hi = sb("q_hi", [P, NS, P], F32R)
        q_lo = sb("q_lo", [P, NS, P], F32R)
        table = sb("table", [1, B * NPP], I32)
        page_i = sb("page_i", [P, B * VCH], I32)
        page_f = sb("page_f", [P, B * VCH])
        slot_of_p = sb("slot_of_p", [P, 1])
        v_row = sb("v_row", [P, B * VCH], I32)
        row_now = sb("row_now", [P, 2, VCH], I32)
        seq_i = sb("seq_i", [P, B], I32)
        seq_f = sb("seq_f", [P, B])
        key = sb("key", [P, CACHED])
        mask = sb("mask", [P, 2, KEYS])
        score = sb("score", [P, 2, KEYS])
        prob = sb("prob", [P, NS, KEYS])
        pn = sb("pn", [P, 2, KEYS])
        top_s = sb("top_s", [P, NS])
        nbias = sb("nbias", [P, NS])
        total = sb("total", [P, NS])
        rtotal = sb("rtotal", [P, NS])
        pT = sb("pT", [P, 2, 5 * P])
        o_out = sb("o_out", [P, 2, HK * P])
        SP_ = [s.ps(f"scores{i}", [P, 2, 512]) for i in range(2)]
        TPa = s.ps("probsT", [P, 5 * P + 384])
        OP = s.ps("outT", [P, 2, 512])

        const_in, seq_cast, mask_zero = sem("const_in"), sem("seq_cast"), sem("mask_zero")
        rows_done, row_set = sem("rows_done"), sem("row_set")
        pool_passed, dve_passed = sem("pool_passed"), sem("dve_passed")
        k_in = [sem("k_in0"), sem("k_in1")]
        v_in = [sem("v_in0"), sem("v_in1")]
        vf_in = [sem("vf_in0"), sem("vf_in1")]
        q_in = [sem("q_in0"), sem("q_in1")]
        khi_done, klo_done, qhi_done, qlo_done = sem("khi_done"), sem("klo_done"), sem("qhi_done"), sem("qlo_done")
        s_done, mask_done, max_done, bias_done = sem("s_done"), sem("mask_done"), sem("max_done"), sem("bias_done")
        exp_done, rec_done, pn_done = sem("exp_done"), sem("rec_done"), sem("pn_done")
        pt_done, pt_evac, pv_done, o_evac = sem("pt_done"), sem("pt_evac"), sem("pv_done"), sem("o_evac")
        o_sent = [sem("o_sent0"), sem("o_sent1")]

        def run(eng, step, lag):
            for j in range(TRIP):
                step(Unit(0, j))
            with eng.Fori(1, UNITS // TRIP) as trip:
                for j in range(TRIP):
                    step(Unit(trip * TRIP, j))
            for j in range(lag):
                step(Unit(UNITS, j))

        def batch(u):
            return (u.base // HK) + u.j // HK

        def trips(u, plus=1):
            return (u.base // TRIP) + (u.j // TRIP + plus)

        block = s.ctx.enter_context(nc.Block())

        @block.sync
        def _(sp):
            sp.dma_start(table[:, :], pages).then_inc(const_in, 16)
            sp.dma_start(seq_i[:, :], seq.partition_broadcast(P)).then_inc(const_in, 16)
            sp.dma_start(key[:, :], iota.partition_broadcast(P)).then_inc(const_in, 16)
            sp.dma_start(slot_of_p[:, :], sidx).then_inc(const_in, 16)
            for g in range(BT):
                sp.dma_start(page_i[g * PSIZE:(g + 1) * PSIZE, :], page_of_chunk[g].partition_broadcast(PSIZE)).then_inc(const_in, 16)
            sp.wait_ge(const_in, CONST)

            def load(par, b, before):
                _, page = nc.values_load_multi_w_load_instructions(table[0:1, bass.ds(b * NPP, NPP)], engines=(mybir.EngineType.SP,),
                                                                   min_val=0, max_val=PAGES - 1,
                                                                   skip_runtime_bounds_check_because="a page number is below PAGES, and the DMA that uses it is checked")
                wait(sp, qlo_done, before)
                sp.dma_start(q_raw[:, par, :], kq_f[bass.ds(b, 1), :, HK * S:].rearrange("o d c -> d (o c)")).then_inc(q_in[par], 16)
                sp.wait_ge(const_in, CONST)
                wait(sp, khi_done, before)
                wait(sp, klo_done, before)
                sp.dma_start(k_raw[:, par, NPP, :], kq_f[bass.ds(b, 1), :, 0:HK * S].rearrange("o d c -> d (o c)")).then_inc(k_in[par], 16)
                for n in range(NPP):
                    sp.dma_start(k_raw[:, par, n, :], kT[bass.ds(page[n], 1)].rearrange("o d c -> d (o c)")).then_inc(k_in[par], 16)
                wait(sp, pv_done, before)
                sp.dma_start(v_fresh[:, par, :], v_f[bass.ds(b, 1)].rearrange("o s c -> s (o c)")).then_inc(vf_in[par], 16)

            def store(par, b, done):
                wait(sp, o_evac, done)
                sp.dma_start(o_f[bass.ds(b, 1)].rearrange("o d c -> d (o c)"), o_out[:, par, :]).then_inc(o_sent[par], 16)

            for par in range(2):
                load(par, par, 0)
            with sp.Fori(1, UNITS // TRIP) as trip:
                for par in range(2):
                    load(par, trip * 2 + par, trip * TRIP + (par - 1) * HK)
                    store(par, trip * 2 + (par - 2), trip * TRIP + (par - 1) * HK)
            for par in range(2):
                store(par, B - 2 + par, UNITS + (par - 1) * HK)
            for par in range(2):
                sp.wait_ge(o_sent[par], 16 * B // 2)

        @block.tensor
        def _(pe):
            def step(u):
                if u.within(UNITS):
                    p2, p4 = u.slot(2), u.slot(NS)
                    wait(pe, klo_done, u.n(1))
                    wait(pe, khi_done, u.n(1))
                    wait(pe, qlo_done, u.n(1))
                    wait(pe, max_done, u.n(-1))
                    for half in range(2):
                        ks = slice(half * HALF, (half + 1) * HALF)
                        out = SP_[p2][:, half, 0:HALF]
                        nc.tensor.matmul(out, q_hi[:, p4, :], k_hi[:, p4, ks], start=True, stop=False)
                        nc.tensor.matmul(out, q_hi[:, p4, :], k_lo[:, p4, ks], start=False, stop=False)
                        mm = nc.tensor.matmul(out, q_lo[:, p4, :], k_hi[:, p4, ks], start=False, stop=True)
                    mm.then_inc(s_done, 1)
                v = u.back(3)
                if v.within(UNITS):
                    wait(pe, pn_done, v.n(1))
                    wait(pe, pt_evac, v.n())
                    for c in range(4):
                        nc.tensor.transpose(TPa[:, c * P:(c + 1) * P], pn[:, v.slot(2), c * P:(c + 1) * P], ident[:, :])
                    nc.tensor.transpose(TPa[0:S, 4 * P:5 * P], pn[:, v.slot(2), CACHED:KEYS], ident[:, :]).then_inc(pt_done, 1)
                w = u.back(4)
                if w.within(UNITS):
                    par, h = (w.j // HK) % 2, w.j % HK
                    hd = slice(h * D, (h + 1) * D)
                    if h == 0:
                        wait(pe, v_in[par], trips(w) * (16 * VCH))
                        wait(pe, vf_in[par], trips(w) * 16)
                    wait(pe, pt_evac, w.n(1))
                    wait(pe, o_evac, w.n(-1))
                    out = OP[:, w.slot(2), 0:P]
                    for c in range(4):
                        nc.tensor.matmul(out, v_raw[:, par, c, hd], pT[:, w.slot(2), c * P:(c + 1) * P], start=(c == 0), stop=False)
                    nc.tensor.matmul(out, v_fresh[:, par, hd], pT[0:S, w.slot(2), 4 * P:5 * P], start=False, stop=True).then_inc(pv_done, 1)

            run(pe, step, 4)

        @block.scalar
        def _(act):
            def step(u):
                v = u.back(3)
                if v.within(UNITS):
                    wait(act, pt_done, v.n(1))
                    wait(act, pv_done, v.n(-1))
                    nc.scalar.copy(pT[:, v.slot(2), 0:4 * P], TPa[:, 0:4 * P])
                    nc.scalar.copy(pT[0:S, v.slot(2), 4 * P:5 * P], TPa[0:S, 4 * P:5 * P]).then_inc(pt_evac, 1)
                if u.within(UNITS):
                    wait(act, bias_done, u.n(1))
                    wait(act, pn_done, u.n(-3))
                    nc.scalar.activation(prob[:, u.slot(NS), :], score[:, u.slot(2), :], ACT.Exp,
                                         bias=nbias[:, u.slot(NS):u.slot(NS) + 1], scale=q_scale[:, bass.ds(u.n(), 1)],
                                         accum_out=total[:, u.slot(NS):u.slot(NS) + 1]).then_inc(exp_done, 1)
                w = u.back(4)
                if w.within(UNITS):
                    par, h = (w.j // HK) % 2, w.j % HK
                    if h == 0:
                        wait(act, o_sent[par], trips(w, 0) * 16)
                    wait(act, pv_done, w.n(1))
                    nc.scalar.copy(o_out[:, par, h * P:(h + 1) * P], OP[:, w.slot(2), 0:P]).then_inc(o_evac, 1)

            run(act, step, 4)

        @block.gpsimd
        def _(pool):
            def gather(b, par, chunks):
                for c in chunks:
                    nc.gpsimd.indirect_dma_start(v_raw[:, par, c, :], None, v_c, bass.IndirectOffsetOnAxis(row_now[:, par, c:c + 1], 0),
                                                 bounds_check=PAGES * PSIZE - 1).then_inc(v_in[par], 16)

            def rows(b, par):
                nc.gpsimd.tensor_copy(row_now[:, par, :], v_row[:, bass.ds(b * VCH, VCH)]).then_inc(row_set, 1)

            pool.wait_ge(rows_done, 1)
            rows(0, 0)
            pool.wait_ge(row_set, 1)
            gather(0, 0, range(VCH))

            def step(u):
                x = u.back(HK)
                if x.within(UNITS - HK) and x.j % HK < 3:
                    h, par = x.j % HK, (x.j // HK + 1) % 2
                    b = batch(x) + 1
                    if h == 0:
                        wait(pool, pv_done, x.n())
                        rows(b, par)
                    else:
                        waits(pool, pool_passed, [(row_set, b + 1), (pv_done, x.n(-h))])
                        gather(b, par, range((h - 1) * VCH // 2, h * VCH // 2))
                if u.within(UNITS):
                    par, h, p4 = (u.j // HK) % 2, u.j % HK, u.slot(NS)
                    landed = [(k_in[par], trips(u) * (16 * NPG))] if h == 0 else []
                    waits(pool, pool_passed, landed + [(s_done, u.n(-3)), (klo_done, u.n(-3))])
                    nc.gpsimd.tensor_scalar(k_hi[:, p4, :].rearrange("p (n c) -> p n c", c=PSIZE),
                                            k_raw[:, par, :, h * PSIZE:(h + 1) * PSIZE], 1.0, 1.0, ALU.mult, ALU.mult).then_inc(khi_done, 1)
                v = u.back(4)
                if v.within(UNITS):
                    waits(pool, pool_passed, [(rec_done, v.n(1)), (pt_done, v.n(-1))])
                    nc.gpsimd.tensor_scalar(pn[:, v.slot(2), :], prob[:, v.slot(NS), :], rtotal[:, v.slot(NS):v.slot(NS) + 1], 1.0,
                                            ALU.mult, ALU.mult).then_inc(pn_done, 1)

            run(pool, step, 4)

        @block.vector
        def _(dve):
            dve.wait_ge(const_in, CONST)
            nc.vector.tensor_scalar(page_f[:, :], page_i[:, :], float(PSIZE), slot_of_p[:, :], ALU.mult, ALU.add).then_inc(seq_cast, 1)
            dve.wait_ge(seq_cast, 1)
            nc.vector.tensor_copy(v_row[:, :], page_f[:, :]).then_inc(rows_done, 1)
            nc.vector.tensor_copy(seq_f[:, :], seq_i[:, :]).then_inc(seq_cast, 1)
            nc.vector.memset(mask[:, :, CACHED:KEYS], 0.0).then_inc(mask_zero, 1)
            dve.wait_ge(seq_cast, 2)
            dve.wait_ge(mask_zero, 1)

            def step(u):
                if u.within(UNITS):
                    par, h, p4 = (u.j // HK) % 2, u.j % HK, u.slot(NS)
                    if h == 0:
                        wait(dve, q_in[par], trips(u) * 16)
                    wait(dve, s_done, u.n(-3))
                    nc.vector.tensor_copy(q_hi[:, p4, :], q_raw[:, par, h * P:(h + 1) * P]).then_inc(qhi_done, 1)
                    wait(dve, khi_done, u.n(1))
                    nc.vector.tensor_tensor(k_lo[:, p4, :].rearrange("p (n c) -> p n c", c=PSIZE),
                                            k_raw[:, par, :, h * PSIZE:(h + 1) * PSIZE],
                                            k_hi[:, p4, :].bitcast(F32).rearrange("p (n c) -> p n c", c=PSIZE), ALU.subtract).then_inc(klo_done, 1)
                    wait(dve, qhi_done, u.n(1))
                    nc.vector.tensor_tensor(q_lo[:, p4, :], q_raw[:, par, h * P:(h + 1) * P], q_hi[:, p4, :].bitcast(F32), ALU.subtract).then_inc(qlo_done, 1)
                v = u.back(2)
                if v.within(UNITS):
                    par, h, p4 = (v.j // HK) % 2, v.j % HK, v.slot(NS)
                    if h == 0:
                        wait(dve, max_done, v.n(-HK))
                        nc.vector.tensor_scalar(mask[:, par, 0:CACHED], key[:, :], seq_f[:, bass.ds(batch(v), 1)], MASKED,
                                                ALU.is_ge, ALU.mult).then_inc(mask_done, 1)
                    masked = [(mask_done, batch(v) + 1)] if h == 0 else []
                    waits(dve, dve_passed, masked + [(s_done, v.n(1)), (exp_done, v.n(-1))])
                    nc.vector.tensor_tensor_reduce(score[:, v.slot(2), :].rearrange("p (a c) -> p a c", a=2), SP_[v.slot(2)][:, :, 0:HALF],
                                                   mask[:, par, :].rearrange("p (a c) -> p a c", a=2), 1.0, -3e38, ALU.add, ALU.max,
                                                   accum_out=top_s[:, p4:p4 + 1]).then_inc(max_done, 1)
                    wait(dve, max_done, v.n(1))
                    nc.vector.tensor_tensor(nbias[:, p4:p4 + 1], top_s[:, p4:p4 + 1], q_nscale[:, bass.ds(v.n(), 1)], ALU.mult).then_inc(bias_done, 1)
                w = u.back(3)
                if w.within(UNITS):
                    p4 = w.slot(NS)
                    wait(dve, exp_done, w.n(1))
                    wait(dve, pn_done, w.n(-3))
                    nc.vector.reciprocal(rtotal[:, p4:p4 + 1], total[:, p4:p4 + 1]).then_inc(rec_done, 1)

            run(dve, step, 3)


def finish(nc, x_tok, woT, cond, mix, o_f, out):
    s = Scope(nc)
    sb, sem = s.sb, s.sem
    with s.ctx:
        o_raw = sb("o_raw", [P, 2, B, R * S])
        w_raw = sb("wo_raw", [P, 2, R, HID])
        o_hi = sb("o_hi", [P, 2, TOK], F32R)
        o_lo = sb("o_lo", [P, 2, TOK], F32R)
        w_hi = sb("wo_hi", [P, 2, HID], F32R)
        w_lo = sb("wo_lo", [P, 2, HID], F32R)
        x_sb = sb("x_sb", [P, TILES, HID])
        y_sb = sb("y_sb", [P, TILES, HID])
        cond_sb = sb("cond_sb", [1, B], I32)
        blocks = sb("blocks", [P, TILES, P])
        Y = [s.ps(f"Y{i}", [P, HID]) for i in range(TILES)]
        o_in = [sem("o_in0"), sem("o_in1")]
        w_in = [sem("wo_in0"), sem("wo_in1")]
        x_in, cond_in, zeroed, mix_in = sem("x_tok_in"), sem("cond_in"), sem("zeroed"), sem("mix_in")
        ohi_done, whi_done, parts_done, head_done = sem("ohi_done"), sem("whi_done"), sem("parts_done"), sem("head_done")
        bank_done, res_done, mix_done, y_done, stored = sem("bank_done"), sem("res_done"), sem("mixed"), sem("y_done"), sem("stored")

        def run(eng, step):
            for j in range(2 * R):
                step(Unit(0, j))
            with eng.Fori(1, HK // 2) as trip:
                for j in range(2 * R):
                    step(Unit(trip * (2 * R), j))

        block = s.ctx.enter_context(nc.Block())

        @block.sync
        def _(sp):
            def load(par, g, before):
                wait(sp, parts_done, before)
                sp.dma_start(o_raw[:, par, :, :], o_f[:, :, bass.ds(g * P, P)].rearrange("b d c -> d b c")).then_inc(o_in[par], 16)
                sp.dma_start(w_raw[:, par, :, :], woT[bass.ds(g, 1)].rearrange("o r p n -> p (o r) n")).then_inc(w_in[par], 16)
            load(0, 0, 0)
            sp.dma_start(cond_sb[:, :], cond).then_inc(cond_in, 16)
            load(1, 1, 0)
            sp.dma_start(x_sb[:, :, :], x_tok.rearrange("(t p) n -> p t n", p=P)).then_inc(x_in, 16)
            sp.wait_ge(cond_in, 16)
            sp.wait_ge(zeroed, 1)
            for b in range(B):
                c = sp.value_load(cond_sb[0:1, b:b + 1], min_val=0, max_val=15)
                q = (b % BT) * S
                sp.dma_start(blocks[q:q + S, b // BT, q:q + S], mix[bass.ds(c, 1)].rearrange("o c d -> c (o d)")).then_inc(mix_in, 16)
            with sp.Fori(1, HK // 2) as trip:
                for par in range(2):
                    load(par, trip * 2 + par, trip * (2 * R) + (par - 1) * R)
            o_tiles = out.rearrange("(t p) n -> t p n", p=P)
            for t in range(TILES):
                sp.wait_ge(y_done, t + 1)
                sp.dma_start(o_tiles[t], y_sb[:, t, :]).then_inc(stored, 16)
            sp.wait_ge(stored, 16 * TILES)

        @block.gpsimd
        def _(pool):
            nc.gpsimd.memset(blocks[:, :, :], 0.0).then_inc(zeroed, 1)

        @block.vector
        def _(dve):
            def step(u):
                par, r, p2 = (u.j // R) % 2, u.j % R, u.slot(2)
                if r == 0:
                    n = ((u.base // (2 * R)) + 1) * 16
                    wait(dve, o_in[par], n)
                    wait(dve, w_in[par], n)
                wait(dve, head_done, u.n(-1))
                src = o_raw[:, par, :, r * S:(r + 1) * S]
                nc.vector.tensor_copy(w_hi[:, p2, :], w_raw[:, par, r, :]).then_inc(whi_done, 1)
                nc.vector.tensor_copy(o_hi[:, p2, :].rearrange("p (b s) -> p b s", s=S), src).then_inc(ohi_done, 1)
                wait(dve, whi_done, u.n(1))
                nc.vector.tensor_tensor(w_lo[:, p2, :], w_raw[:, par, r, :], w_hi[:, p2, :].bitcast(F32), ALU.subtract)
                wait(dve, ohi_done, u.n(1))
                nc.vector.tensor_tensor(o_lo[:, p2, :].rearrange("p (b s) -> p b s", s=S), src,
                                        o_hi[:, p2, :].bitcast(F32).rearrange("p (b s) -> p b s", s=S), ALU.subtract).then_inc(parts_done, 1)

            run(dve, step)
            dve.wait_ge(x_in, 16)
            for t in range(TILES):
                dve.wait_ge(bank_done, t + 1)
                nc.vector.tensor_tensor(x_sb[:, t, :], x_sb[:, t, :], Y[t][:, :], ALU.add).then_inc(res_done, 1)
            for t in range(TILES):
                dve.wait_ge(mix_done, t + 1)
                nc.vector.tensor_tensor(y_sb[:, t, :], x_sb[:, t, :], Y[t][:, :], ALU.add).then_inc(y_done, 1)

        @block.tensor
        def _(pe):
            def step(u):
                p2 = u.slot(2)
                first = u.static() and u.n() == 0
                wait(pe, parts_done, u.n(1))
                for t in range(TILES):
                    cols = slice(t * P, (t + 1) * P)
                    nc.tensor.matmul(Y[t][:, :], o_hi[:, p2, cols], w_hi[:, p2, :], start=first, stop=False, skip_group_check=True)
                    nc.tensor.matmul(Y[t][:, :], o_hi[:, p2, cols], w_lo[:, p2, :], start=False, stop=False, skip_group_check=True)
                    mm = nc.tensor.matmul(Y[t][:, :], o_lo[:, p2, cols], w_hi[:, p2, :], start=False, stop=True, skip_group_check=True)
                mm.then_inc(head_done, 1)

            run(pe, step)
            pe.wait_ge(head_done, HQ)
            pe.sem_inc(bank_done, TILES)
            pe.wait_ge(mix_in, 16 * B)
            for t in range(TILES):
                pe.wait_ge(res_done, t + 1)
                nc.tensor.matmul(Y[t][:, :], blocks[:, t, :], x_sb[:, t, :], start=True, stop=True).then_inc(mix_done, 1)


def program(nc, xT, x_tok, w_all, woT, seq, seq_tile, pages, page_of_chunk, cond, q_w, k_w, kT, v_c, mix, inv_freq, sidx, iota, eye, out):
    kq_f = nc.dram_tensor("kq_fresh", [B, D, HK * S + HK * P], F32).ap()
    v_f = nc.dram_tensor("v_fresh_all", [B, S, HK * D], F32).ap()
    o_f = nc.dram_tensor("heads_out", [B, D, HK * P], F32).ap()
    top = Scope(nc)
    with top.ctx:
        ident = top.sb("ident", [P, P])
        q_scale = top.sb("q_scale", [P, UNITS])
        q_nscale = top.sb("q_nscale", [P, UNITS])
        project(nc, top, xT, w_all, seq_tile, inv_freq, sidx, q_w, k_w, kq_f, v_f.rearrange("b s c -> (b s) c"), eye, ident, q_scale, q_nscale)
        attend(nc, seq, pages, page_of_chunk, sidx, kT, v_c, iota, kq_f, v_f, o_f, ident, q_scale, q_nscale)
        finish(nc, x_tok, woT, cond, mix, o_f, out)


def kernel(**inputs):
    import concourse.bacc as _bacc
    from concourse.bass_utils import run_bass_kernel_spmd as _run

    a = {k: np.asarray(v) for k, v in inputs.items()}
    cont = np.ascontiguousarray
    x = a["x"].reshape(TOK, HID)
    w_all = np.concatenate([a["L0_cond_Wv"], a["L0_cond_Wk"], a["L0_cond_Wq"]], axis=0)
    half = np.arange(0, D, 2, dtype=np.float32) / np.float32(D)
    arrays = {
        "xT": cont(x.T.reshape(KC, P, TOK).transpose(1, 0, 2)),
        "x_tok": cont(x),
        "w_all": cont(w_all.reshape(CHUNKS, NC_, KC, P).transpose(0, 3, 2, 1)),
        "woT": cont(a["L0_cond_Wo"].T.reshape(HK, R, P, HID)),
        "seq": cont(a["itok_B_207_1644"]),
        "seq_tile": cont(a["itok_B_207_1644"].reshape(TILES, BT).T.reshape(-1)),
        "pages": cont(a["itok_Bx16_0_63"].reshape(1, B * NPP)),
        "page_of_chunk": cont(a["itok_Bx16_0_63"].reshape(B * VCH, BT).T),
        "cond": cont(a["itok_B_0_15"].reshape(1, B)),
        "q_w": cont(a["L0_cond_q_norm_w"]),
        "k_w": cont(a["L0_cond_k_norm_w"]),
        "kT": cont(a["L0_cond_k_cache"].transpose(0, 3, 2, 1).reshape(PAGES, D, HK * PSIZE)),
        "v_c": cont(a["L0_cond_v_cache"].reshape(PAGES * PSIZE, HK * D)),
        "mix": cont(a["L1_cond_weights"]),
        "inv_freq": (np.float32(1) / (10000.0 ** half.astype(np.float64)).astype(np.float32)).astype(np.float32),
        "sidx": (np.arange(P) % S).astype(np.float32).reshape(P, 1),
        "iota": np.arange(CACHED).astype(np.float32),
        "eye": np.eye(P, dtype=np.float32),
    }
    nc = _bacc.Bacc("TRN2", target_bir_lowering=False, num_devices=1)
    args = [nc.dram_tensor(f"in_{k}", v.shape, mybir.dt.from_np(v.dtype), kind="ExternalInput").ap() for k, v in arrays.items()]
    out = nc.dram_tensor("out_y", [TOK, HID], F32, kind="ExternalOutput").ap()
    program(nc, *args, out)
    r = _run(nc, [{f"in_{k}": v for k, v in arrays.items()}], core_ids=[0])
    return r.results[0]["out_y"].reshape(B, S, HID)
```

```python
from contextlib import ExitStack

import numpy as np
import concourse.bass as bass
from concourse import mybir

F32 = mybir.dt.float32
F32R = mybir.dt.float32r
I32 = mybir.dt.int32
ALU = mybir.AluOpType
ACT = mybir.ActivationFunctionType
AX = mybir.AxisListType

P = 128
B, S, HID = 32, 32, 512
D, HQ, HK = 128, 32, 8
R = HQ // HK
PAGES, PSIZE, NPP = 64, 32, 16
CACHED = NPP * PSIZE
KEYS = CACHED + S
HALF = KEYS // 2
NPG = NPP + 1
TOK = B * S
TILES = TOK // P
BT = P // S
KC = HID // P
NC_ = 512
CHUNKS = 2 * HK * D // NC_ + HQ * D // NC_
EPS = 1e-6
SCALE = 1.0 / float(np.sqrt(D))
MASKED = -1e30
UNITS = B * HK
ATTN_IN = 16 * (3 + BT)
VCH = CACHED // P
TRIP = 16
MAGIC = 1.5 * 2.0 ** 23
PI2_A = 6.28125
PI2_B = float(np.float32(np.floor((2 * np.pi - PI2_A) * 2.0 ** 20) / 2.0 ** 20))
PI2_C = float(np.float32(2 * np.pi - PI2_A - PI2_B))


class Unit:

    def __init__(self, base, j):
        self.base, self.j = base, j

    def back(self, n):
        return Unit(self.base, self.j - n)

    def n(self, plus=0):
        return self.base + (self.j + plus)

    def static(self):
        return isinstance(self.base, int)

    def within(self, end):
        return not self.static() or 0 <= self.n() < end

    def slot(self, k):
        return self.j % k


def wait(eng, sem, value):
    if not isinstance(value, int) or value > 0:
        eng.wait_ge(sem, value)


def waits(eng, passed, pairs):
    for sem, v in pairs:
        wait(eng, sem, v)
    eng.sem_inc(passed, 1)


class Scope:
    def __init__(self, nc):
        self.nc, self.ctx = nc, ExitStack()

    def sb(self, name, shape, dt=F32):
        return self.ctx.enter_context(self.nc.sbuf_tensor(name, shape, dt))

    def ps(self, name, shape, dt=F32):
        return self.ctx.enter_context(self.nc.psum_tensor(name, shape, dt))

    def sem(self, name):
        return self.ctx.enter_context(self.nc.semaphore(name))


class Shared(Scope):

    def __init__(self, nc):
        super().__init__(nc)
        sb, sem = self.sb, self.sem
        self.ident = sb("ident", [P, P])
        self.q_scale = sb("q_scale", [P, UNITS])
        self.q_nscale = sb("q_nscale", [P, UNITS])
        self.table = sb("table", [1, B * NPP], I32)
        self.page_i = sb("page_i", [P, B * VCH], I32)
        self.slot_of_p = sb("slot_of_p", [P, 1])
        self.v_row = sb("v_row", [P, B * VCH], I32)
        self.row_now = sb("row_now", [P, 2, VCH], I32)
        self.seq_i = sb("seq_i", [P, B], I32)
        self.key = sb("key", [P, CACHED])
        self.k_raw = sb("k_raw", [P, 2, NPG, HK * PSIZE])
        self.v_raw = sb("v_raw", [P, 2, VCH, HK * D])
        self.o_raw = sb("o_raw", [P, 2, B, R * S])
        self.wo_raw = sb("wo_raw", [P, 2, R, HID])
        self.attn_in, self.rows_done, self.row_set = sem("attn_in"), sem("rows_done"), sem("row_set")
        self.k_in = [sem("k_in0"), sem("k_in1")]
        self.v_in = [sem("v_in0"), sem("v_in1")]
        self.o_in = [sem("o_in0"), sem("o_in1")]
        self.wo_in = [sem("wo_in0"), sem("wo_in1")]


def page_numbers(nc, table, b):
    return nc.values_load_multi_w_load_instructions(table[0:1, bass.ds(b * NPP, NPP)], engines=(mybir.EngineType.SP,),
                                                    min_val=0, max_val=PAGES - 1,
                                                    skip_runtime_bounds_check_because="a page number is below PAGES, and the DMA that uses it is checked")[1]


def gather_values(nc, sh, v_c, par, chunks):
    for c in chunks:
        nc.gpsimd.indirect_dma_start(sh.v_raw[:, par, c, :], None, v_c, bass.IndirectOffsetOnAxis(sh.row_now[:, par, c:c + 1], 0),
                                     bounds_check=PAGES * PSIZE - 1).then_inc(sh.v_in[par], 16)


def place_rows(nc, sh, b, par):
    nc.gpsimd.tensor_copy(sh.row_now[:, par, :], sh.v_row[:, bass.ds(b * VCH, VCH)]).then_inc(sh.row_set, 1)


def heads4(ap):
    return ap.rearrange("p (h d) -> p h d", d=D)


def project(nc, sh, xT, w_all, seq_tile, seq, inv_freq, sidx, q_w, k_w, pages, page_of_chunk, kT, v_c, iota, ident_d, kq_f, v_f):
    s = Scope(nc)
    sb, sem = s.sb, s.sem
    with s.ctx:
        def part(buf, at, n, shape, names):
            dims = dict(zip(names[:-1], shape))
            flat = buf.rearrange("p a b -> p (a b)")[:, at:at + n]
            return flat.rearrange("p (%s) -> p %s" % (" ".join(names), " ".join(names)), **dims)

        k0, k1, v1 = sh.k_raw[:, 0, :, :], sh.k_raw[:, 1, :, :], sh.v_raw[:, 1, :, :]
        spare = sh.o_raw[:, :, :, :].rearrange("p a b c -> p a (b c)")
        TD, TH = TILES * D, TILES * D // 2
        x_raw = part(k0, 0, KC * TOK, [KC], "kt")
        ident = sh.ident
        x_hi = sb("x_hi", [P, KC, TOK], F32R)
        x_lo = sb("x_lo", [P, KC, TOK], F32R)
        w_raw = sh.wo_raw
        w_hi = sb("w_hi", [P, 2, KC, NC_], F32R)
        w_lo = sb("w_lo", [P, 2, KC, NC_], F32R)
        pos_i = sb("pos_i", [P, TILES], I32)
        pos_f = sb("pos_f", [P, TILES])
        inv = sb("inv", [P, D // 2])
        wb = sb("wb", [P, 2, D])
        ang = part(k1, 0, TH, [TILES], "td")
        turn = part(k1, TH, TH, [TILES], "td")
        sin_t = part(k1, 2 * TH, TH, [TILES], "td")
        cos_t = part(k1, 3 * TH, TH, [TILES], "td")
        rope_c = part(v1, 0, 2 * TD, [2, TILES], "qtd")
        rope_s = part(v1, 2 * TD, 2 * TD, [2, TILES], "qtd")
        sq = part(spare, 0, 2 * NC_, [2], "sn")
        raw = part(spare, 2 * NC_, 2 * NC_, [2], "sn")
        m1 = part(spare, 4 * NC_, 2 * NC_, [2], "sn")
        m2 = part(spare, 6 * NC_, 2 * NC_, [2], "sn")
        rp = part(spare, 8 * NC_, 4 * NC_, [4], "sn")
        outb = part(spare, 12 * NC_, 4 * NC_, [4], "sn")
        page_f = sb("page_f", [P, B * VCH])
        ss = sb("ss", [P, 2, 4])
        ms = sb("ms", [P, 2, 4])
        k_rs = sb("k_rs", [P, 2, 4])
        q_rs = sb("q_rs", [P, TILES, HQ])
        minus_half = sb("minus_half", [P, 4])
        QP = [s.ps(f"QP{i}", [P, NC_]) for i in range(4)]
        TP = [s.ps(f"TP{i}", [P, NC_]) for i in range(4)]

        x_in, w0_in = [sem(f"x_in{k}") for k in range(KC)], [sem(f"w0_in{k}") for k in range(KC)]
        small_in, ident_in, page_cast = sem("small_in"), sem("ident_in"), sem("page_cast")
        w_in = [sem("w_in0"), sem("w_in1")]
        x_hi_done, x_split = sem("x_hi_done"), sem("x_split")
        w0_hi_done, w0_split = sem("w0_hi_done"), sem("w0_split")
        w_hi_done, w_split = sem("w_hi_done"), sem("w_split")
        tab, trig = sem("tab"), sem("trig")
        mm_done, qp_read, m1_done = sem("mm_done"), sem("qp_read"), sem("m1_done")
        sq_done = sem("sq_done")
        ss_done, ms_done, rs_done = sem("ss_done"), sem("ms_done"), sem("rs_done")
        m2_done, add_done, rp_done = sem("m2_done"), sem("add_done"), sem("rp_done")
        t_done, t_evac = sem("t_done"), sem("t_evac")
        out_sent = [sem(f"out_sent{i}") for i in range(4)]
        const_set, table_step, scale_moved = sem("const_set"), sem("table_step"), sem("scale_moved")

        KU = 2 * TILES
        NU = CHUNKS * TILES

        def kind(u):
            if not u.static():
                return "q"
            return "v" if u.n() < KU else "k" if u.n() < 2 * KU else "q"

        def turned(u):
            return u.n(-KU)

        def run(eng, step, lag):
            pairs = NU // TRIP
            for pair in range(2):
                for j in range(TRIP):
                    step(Unit(pair * TRIP, j))
            with eng.Fori(2, pairs - 1) as pair:
                for j in range(TRIP):
                    step(Unit(pair * TRIP, j))
            for j in range(TRIP + lag):
                step(Unit((pairs - 1) * TRIP, j))

        block = s.ctx.enter_context(nc.Block())

        @block.sync
        def _(sp):
            for k in range(KC):
                sp.dma_start(x_raw[:, k, :], xT[:, k, :]).then_inc(x_in[k], 16)
                sp.dma_start(w_raw[:, 0, k, :], w_all[0][:, k, :]).then_inc(w0_in[k], 16)
            for bl in range(BT):
                src = seq_tile[bl * TILES:(bl + 1) * TILES].partition_broadcast(S)
                sp.dma_start(pos_i[bl * S:(bl + 1) * S, :], src).then_inc(small_in, 16)
            sp.dma_start(sh.slot_of_p[:, :], sidx).then_inc(small_in, 16)
            sp.dma_start(inv[:, :], inv_freq.partition_broadcast(P)).then_inc(small_in, 16)
            sp.dma_start(wb[:, 0, :], q_w.partition_broadcast(P)).then_inc(small_in, 16)
            sp.dma_start(wb[:, 1, :], k_w.partition_broadcast(P)).then_inc(small_in, 16)
            sp.dma_start(ident[:, :], ident_d).then_inc(ident_in, 16)
            sp.dma_start(w_raw[:, 1, :, :], w_all[1]).then_inc(w_in[1], 16)
            for g in range(BT):
                sp.dma_start(sh.page_i[g * PSIZE:(g + 1) * PSIZE, :], page_of_chunk[g].partition_broadcast(PSIZE)).then_inc(sh.attn_in, 16)
            sp.dma_start(sh.table[:, :], pages).then_inc(sh.attn_in, 16)
            sp.dma_start(sh.seq_i[:, :], seq.partition_broadcast(P)).then_inc(sh.attn_in, 16)
            sp.dma_start(sh.key[:, :], iota.partition_broadcast(P)).then_inc(sh.attn_in, 16)
            early_page = [None] * NPP

            def early_pages(u):
                b, n = (u.n() - TRIP) // 8, u.j % 8 * 2
                if n == 0:
                    if b == 0:
                        sp.wait_ge(sh.attn_in, ATTN_IN)
                        sp.wait_ge(x_split, KC)
                    else:
                        sp.wait_ge(tab, 2)
                    early_page[:] = page_numbers(nc, sh.table, b)
                for i in (n, n + 1):
                    sp.dma_start(sh.k_raw[:, b, i, :], kT[bass.ds(early_page[i], 1)].rearrange("o d c -> d (o c)")).then_inc(sh.k_in[b], 16)

            def step(u):
                if u.static() and TRIP <= u.n() < 2 * TRIP:
                    early_pages(u)
                if u.slot(TILES) == 2 and (not u.static() or u.n() // TILES + 2 < CHUNKS):
                    chunk = Unit(u.base // TILES, u.j // TILES)
                    slot = (u.j // TILES) % 2
                    if chunk.static() and chunk.n() == 0:
                        sp.wait_ge(w0_split, KC)
                    wait(sp, w_split, chunk.n())
                    sp.dma_start(w_raw[:, slot, :, :], w_all[bass.ds(chunk.n(2), 1)].rearrange("o p k n -> p (o k) n")).then_inc(w_in[slot], 16)
                v = u.back(2)
                if not v.within(NU):
                    return
                o = v.slot(4)
                wait(sp, t_evac, v.n(1))
                tile = v.j % TILES
                if kind(v) == "v":
                    chunk = v.n() // TILES
                    dst = v_f[tile * P:(tile + 1) * P, chunk * NC_:(chunk + 1) * NC_]
                    src = outb[:, o, :]
                else:
                    col = (v.base // TILES + (v.j // TILES - 2)) * P
                    dst = kq_f[tile * BT:(tile + 1) * BT, :, bass.ds(col, P)].rearrange("b d c -> d b c")
                    src = outb[:, o, :].rearrange("p (b c) -> p b c", b=BT)
                sp.dma_start(dst, src).then_inc(out_sent[o], 16)

            run(sp, step, 2)
            for o in range(4):
                sp.wait_ge(out_sent[o], 16 * NU // 4)

        @block.tensor
        def _(pe):
            def step(u):
                if u.within(NU):
                    if u.slot(TILES) == 0:
                        wait(pe, w_split, u.base // TILES + u.j // TILES)
                    wait(pe, qp_read, u.n(-3))
                    tile, slot = u.j % TILES, (u.j // TILES) % 2
                    cols = slice(tile * P, (tile + 1) * P)
                    bank = QP[u.slot(4)]
                    for k in range(KC):
                        if u.static() and u.n() == 0:
                            pe.wait_ge(x_split, k + 1)
                            pe.wait_ge(w0_split, k + 1)
                        nc.tensor.matmul(bank[:, :], x_hi[:, k, cols], w_hi[:, slot, k, :], start=(k == 0), stop=False)
                        nc.tensor.matmul(bank[:, :], x_hi[:, k, cols], w_lo[:, slot, k, :], start=False, stop=False)
                        mm = nc.tensor.matmul(bank[:, :], x_lo[:, k, cols], w_hi[:, slot, k, :], start=False, stop=(k == KC - 1))
                    mm.then_inc(mm_done, 1)
                v = u.back(2)
                if v.within(NU) and kind(v) != "v":
                    if v.static() and v.n() == KU:
                        pe.wait_ge(ident_in, 16)
                    wait(pe, rp_done, turned(v) + 1)
                    wait(pe, t_evac, v.n(-3))
                    for h in range(4):
                        tr = nc.tensor.transpose(TP[v.slot(4)][:, h * P:(h + 1) * P], rp[:, v.slot(4), h * D:(h + 1) * D], ident[:, :])
                    tr.then_inc(t_done, 1)

            run(pe, step, 2)

        @block.scalar
        def _(act):
            for k in range(KC):
                act.wait_ge(x_in[k], 16)
                nc.scalar.copy(x_hi[:, k, :], x_raw[:, k, :]).then_inc(x_hi_done, 1)
                act.wait_ge(w0_in[k], 16)
                nc.scalar.copy(w_hi[:, 0, k, :], w_raw[:, 0, k, :]).then_inc(w0_hi_done, 1)

            def step(u):
                if u.static() and u.n() == 4:
                    act.wait_ge(tab, 1)
                    nc.scalar.activation(sin_t, sin_t, ACT.Sin).then_inc(trig, 1)
                    nc.scalar.activation(cos_t, cos_t, ACT.Sin).then_inc(trig, 1)
                if u.within(NU):
                    bank = QP[u.slot(4)]
                    wait(act, mm_done, u.n(1))
                    if kind(u) == "v":
                        o = u.slot(4)
                        wait(act, out_sent[o], u.n(-o) * 4)
                        nc.scalar.copy(outb[:, o, :], bank[:, :]).then_inc(qp_read, 1)
                    else:
                        wait(act, ss_done, turned(u) - 1)
                        nc.scalar.activation(sq[:, u.slot(2), :], bank[:, :], ACT.Square).then_inc(sq_done, 1)
                        wait(act, m1_done, turned(u) - 1)
                        wait(act, m2_done, turned(u) - 1)
                        nc.scalar.copy(raw[:, u.slot(2), :], bank[:, :]).then_inc(qp_read, 1)
                v = u.back(2)
                if v.within(NU):
                    if kind(v) == "v":
                        wait(act, qp_read, v.n(1))
                        act.sem_inc(t_evac, 1)
                    else:
                        o = v.slot(4)
                        wait(act, t_done, turned(v) + 1)
                        wait(act, out_sent[o], v.n(-o) * 4)
                        dst = outb[:, o, :].rearrange("p (b r s) -> p r b s", b=BT, r=4)
                        src = TP[v.slot(4)][:, :].rearrange("p (r b s) -> p r b s", b=BT, r=4)
                        nc.scalar.copy(dst, src).then_inc(t_evac, 1)

            run(act, step, 2)

        @block.gpsimd
        def _(pool):
            nc.gpsimd.memset(minus_half[:, :], -0.5).then_inc(const_set, 1)
            pool.wait_ge(const_set, 1)

            def step(u):
                if kind(u) == "v":
                    return
                n, p2, qk = turned(u), u.slot(2), int(kind(u) == "k")
                tile = u.j % TILES
                wait(pool, qp_read, u.n(1))
                wait(pool, rp_done, n - 1)
                r, o = heads4(raw[:, p2, :]), heads4(m2[:, p2, :])
                for half in range(2):
                    a, c = half * 64, (1 - half) * 64
                    tt = nc.gpsimd.tensor_tensor(o[:, :, a:a + 64], r[:, :, c:c + 64],
                                                 rope_s[:, qk, tile:tile + 1, a:a + 64].to_broadcast([P, 4, 64]), ALU.mult)
                tt.then_inc(m2_done, 1)
                wait(pool, ms_done, n + 1)
                if qk:
                    rs = k_rs[:, p2, :]
                else:
                    rs = q_rs[:, tile, bass.ds((u.base // TILES + (u.j // TILES - 4)) * 4, 4)]
                nc.gpsimd.tensor_tensor(rs, ms[:, p2, :], minus_half[:, :], ALU.pow).then_inc(rs_done, 1)

            pool.wait_ge(sh.rows_done, 1)
            place_rows(nc, sh, 0, 0)
            pool.wait_ge(sh.row_set, 1)
            pool.wait_ge(tab, 2)
            gather_values(nc, sh, v_c, 0, range(VCH))
            run(pool, step, 0)

        @block.vector
        def _(dve):
            link = [0]

            def then(ins):
                link[0] += 1
                ins.then_inc(table_step, 1)
                dve.wait_ge(table_step, link[0])

            def split_w_piece(slot, k, part, chunk):
                if part == 0:
                    nc.vector.tensor_copy(w_hi[:, slot, k, :], w_raw[:, slot, k, :]).then_inc(w_hi_done, 1)
                else:
                    wait(dve, w_hi_done, chunk.n(-1) * KC + (k + 1))
                    ins = nc.vector.tensor_tensor(w_lo[:, slot, k, :], w_raw[:, slot, k, :], w_hi[:, slot, k, :].bitcast(F32), ALU.subtract)
                    if k == KC - 1:
                        ins.then_inc(w_split, 1)

            for k in range(KC):
                dve.wait_ge(x_hi_done, k + 1)
                nc.vector.tensor_tensor(x_lo[:, k, :], x_raw[:, k, :], x_hi[:, k, :].bitcast(F32), ALU.subtract).then_inc(x_split, 1)
                dve.wait_ge(w0_hi_done, k + 1)
                nc.vector.tensor_tensor(w_lo[:, 0, k, :], w_raw[:, 0, k, :], w_hi[:, 0, k, :].bitcast(F32), ALU.subtract).then_inc(w0_split, 1)
            dve.wait_ge(small_in, 16 * (BT + 4))
            then(nc.vector.tensor_copy(pos_f[:, :], pos_i[:, :]))
            then(nc.vector.tensor_scalar(pos_f[:, :], pos_f[:, :], sh.slot_of_p[:, :], None, ALU.add))
            then(nc.vector.tensor_tensor(ang[:, :, :], pos_f[:, :].unsqueeze(2).to_broadcast([P, TILES, D // 2]),
                                         inv[:, :].unsqueeze(1).to_broadcast([P, TILES, D // 2]), ALU.mult))
            for t, off in ((sin_t, 0.0), (cos_t, 0.25)):
                then(nc.vector.tensor_scalar(turn[:, :, :], ang[:, :, :], 1 / (2 * np.pi), off, ALU.mult, ALU.add))
                then(nc.vector.tensor_scalar(turn[:, :, :], turn[:, :, :], MAGIC, MAGIC, ALU.add, ALU.subtract))
                then(nc.vector.scalar_tensor_tensor(t[:, :, :], turn[:, :, :], -PI2_A, ang[:, :, :], ALU.mult, ALU.add))
                then(nc.vector.scalar_tensor_tensor(t[:, :, :], turn[:, :, :], -PI2_B, t[:, :, :], ALU.mult, ALU.add))
                then(nc.vector.scalar_tensor_tensor(t[:, :, :], turn[:, :, :], -PI2_C, t[:, :, :], ALU.mult, ALU.add))
                if off:
                    then(nc.vector.tensor_scalar(t[:, :, :], t[:, :, :], float(np.pi / 2), None, ALU.add))
                then(nc.vector.tensor_scalar(t[:, :, :], t[:, :, :], 3.1415925, -3.1415925, ALU.min, ALU.max))
            nc.vector.memset(ms[:, :, :], 0.0).then_inc(tab, 1)
            dve.wait_ge(sh.attn_in, ATTN_IN)
            nc.vector.tensor_scalar(page_f[:, :], sh.page_i[:, :], float(PSIZE), sh.slot_of_p[:, :], ALU.mult, ALU.add).then_inc(page_cast, 1)
            dve.wait_ge(page_cast, 1)
            nc.vector.tensor_copy(sh.v_row[:, :], page_f[:, :]).then_inc(sh.rows_done, 1)

            def rope_tables():
                dve.wait_ge(trig, 2)
                for qk in range(2):
                    w1 = wb[:, qk:qk + 1, 0:64].to_broadcast([P, TILES, 64])
                    w2 = wb[:, qk:qk + 1, 64:128].to_broadcast([P, TILES, 64])
                    nc.vector.tensor_tensor(rope_c[:, qk, :, 0:64], cos_t[:, :, :], w1, ALU.mult)
                    nc.vector.tensor_tensor(rope_c[:, qk, :, 64:128], cos_t[:, :, :], w2, ALU.mult)
                    nc.vector.scalar_tensor_tensor(rope_s[:, qk, :, 0:64], sin_t[:, :, :], -1.0, w2, ALU.mult, ALU.mult)
                    last = nc.vector.tensor_tensor(rope_s[:, qk, :, 64:128], sin_t[:, :, :], w1, ALU.mult)
                last.then_inc(tab, 1)
                dve.wait_ge(tab, 2)

            def step(u):
                if u.static() and u.n() == 6:
                    rope_tables()
                p2, tile = u.slot(2), u.j % TILES
                if kind(u) != "v":
                    n, qk = turned(u), int(kind(u) == "k")
                    wait(dve, qp_read, u.n(1))
                    wait(dve, rp_done, n - 1)
                    nc.vector.tensor_tensor(heads4(m1[:, p2, :]), heads4(raw[:, p2, :]),
                                            rope_c[:, qk, tile:tile + 1, :].to_broadcast([P, 4, D]), ALU.mult).then_inc(m1_done, 1)
                nxt = Unit(u.base // TILES, u.j // TILES + 1)
                if not nxt.static() or nxt.n() < CHUNKS:
                    slot = (u.j // TILES + 1) % 2
                    if tile == 0:
                        wait(dve, w_in[slot], (nxt.base // 2 + (nxt.j // 2 + slot)) * 16)
                        wait(dve, mm_done, u.n())
                    split_w_piece(slot, tile // 2, tile % 2, nxt)
                if kind(u) == "v":
                    return
                wait(dve, sq_done, n + 1)
                wait(dve, rs_done, n - 1)
                nc.vector.reduce_sum(ss[:, p2, :], heads4(sq[:, p2, :]), AX.X).then_inc(ss_done, 1)
                wait(dve, ss_done, n + 1)
                nc.vector.tensor_scalar(ms[:, p2, :], ss[:, p2, :], 1.0 / D, EPS, ALU.mult, ALU.add).then_inc(ms_done, 1)
                wait(dve, m2_done, n + 1)
                wait(dve, m1_done, n + 1)
                wait(dve, t_done, n - 3)
                if qk:
                    nc.vector.tensor_tensor(m1[:, p2, :], m1[:, p2, :], m2[:, p2, :], ALU.add).then_inc(add_done, 1)
                    wait(dve, add_done, n + 1)
                    wait(dve, rs_done, n + 1)
                    nc.vector.tensor_tensor(heads4(rp[:, u.slot(4), :]), heads4(m1[:, p2, :]),
                                            k_rs[:, p2, :].unsqueeze(2).to_broadcast([P, 4, D]), ALU.mult).then_inc(rp_done, 1)
                else:
                    nc.vector.tensor_tensor(rp[:, u.slot(4), :], m1[:, p2, :], m2[:, p2, :], ALU.add).then_inc(rp_done, 1)

            run(dve, step, 0)
            dve.wait_ge(rs_done, (CHUNKS - 2) * TILES)
            qs = sh.q_scale[:, :].rearrange("p (t b k) -> p t b k", b=BT, k=HK)
            qr = q_rs[:, :, :].rearrange("p t (k r) -> p t k r", r=R)
            for bl in range(BT):
                for r in range(R):
                    last = nc.vector.tensor_scalar(qs[r * S:(r + 1) * S, :, bl, :], qr[bl * S:(bl + 1) * S, :, :, r], SCALE, None, ALU.mult)
            last.then_inc(scale_moved, 1)
            dve.wait_ge(scale_moved, 1)
            nc.vector.tensor_scalar(sh.q_nscale[:, :], sh.q_scale[:, :], -1.0, None, ALU.mult)


def attend(nc, sh, kT, v_c, kq_f, v_f, o_f, woT):
    s = Scope(nc)
    sb, sem = s.sb, s.sem
    with s.ctx:
        NS = 4
        k_raw, v_raw, ident, q_scale = sh.k_raw, sh.v_raw, sh.ident, sh.q_scale
        k_in, v_in = sh.k_in, sh.v_in
        v_fresh = sb("v_fresh", [S, 2, HK * D])
        q_raw = sb("q_raw", [P, 2, HK * P])
        k_hi = sb("k_hi", [P, NS, KEYS], F32R)
        k_lo = sb("k_lo", [P, NS, KEYS], F32R)
        q_hi = sb("q_hi", [P, NS, P], F32R)
        q_lo = sb("q_lo", [P, NS, P], F32R)
        seq_f = sb("seq_f", [P, B])
        mask = sb("mask", [P, 2, KEYS])
        score = sb("score", [P, 2, KEYS])
        prob = sb("prob", [P, NS, KEYS])
        pn = sb("pn", [P, 2, KEYS])
        top_s = sb("top_s", [P, NS])
        nbias = sb("nbias", [P, NS])
        total = sb("total", [P, NS])
        rtotal = sb("rtotal", [P, NS])
        pT = sb("pT", [P, 2, 5 * P])
        o_out = sb("o_out", [P, 2, HK * P])
        SP_ = [s.ps(f"scores{i}", [P, 2, 512]) for i in range(2)]
        TPa = s.ps("probsT", [P, 5 * P + 384])
        OP = s.ps("outT", [P, 2, 512])

        seq_cast, mask_zero = sem("seq_cast"), sem("mask_zero")
        pool_passed, dve_passed = sem("pool_passed"), sem("dve_passed")
        vf_in = [sem("vf_in0"), sem("vf_in1")]
        q_in = [sem("q_in0"), sem("q_in1")]
        khi_done, klo_done, qhi_done, qlo_done = sem("khi_done"), sem("klo_done"), sem("qhi_done"), sem("qlo_done")
        s_done, mask_done, max_done, bias_done = sem("s_done"), sem("mask_done"), sem("max_done"), sem("bias_done")
        exp_done, rec_done, pn_done = sem("exp_done"), sem("rec_done"), sem("pn_done")
        pt_done, pt_evac, pv_done, o_evac = sem("pt_done"), sem("pt_evac"), sem("pv_done"), sem("o_evac")
        o_sent = [sem("o_sent0"), sem("o_sent1")]

        def run(eng, step, lag):
            for j in range(TRIP):
                step(Unit(0, j))
            with eng.Fori(1, UNITS // TRIP) as trip:
                for j in range(TRIP):
                    step(Unit(trip * TRIP, j))
            for j in range(lag):
                step(Unit(UNITS, j))

        def batch(u):
            return (u.base // HK) + u.j // HK

        def trips(u, plus=1):
            return (u.base // TRIP) + (u.j // TRIP + plus)

        block = s.ctx.enter_context(nc.Block())

        @block.sync
        def _(sp):
            def load_fresh(par, b, before):
                wait(sp, qlo_done, before)
                sp.dma_start(q_raw[:, par, :], kq_f[bass.ds(b, 1), :, HK * S:].rearrange("o d c -> d (o c)")).then_inc(q_in[par], 16)
                sp.wait_ge(sh.attn_in, ATTN_IN)
                wait(sp, khi_done, before)
                wait(sp, klo_done, before)
                sp.dma_start(k_raw[:, par, NPP, :], kq_f[bass.ds(b, 1), :, 0:HK * S].rearrange("o d c -> d (o c)")).then_inc(k_in[par], 16)

            def load_fresh_v(par, b, before):
                wait(sp, pv_done, before)
                sp.dma_start(v_fresh[:, par, :], v_f[bass.ds(b, 1)].rearrange("o s c -> s (o c)")).then_inc(vf_in[par], 16)

            def load_pages(par, page):
                for n in range(NPP):
                    sp.dma_start(k_raw[:, par, n, :], kT[bass.ds(page[n], 1)].rearrange("o d c -> d (o c)")).then_inc(k_in[par], 16)

            def store(par, b, done):
                wait(sp, o_evac, done)
                sp.dma_start(o_f[bass.ds(b, 1)].rearrange("o d c -> d (o c)"), o_out[:, par, :]).then_inc(o_sent[par], 16)

            def load_heads(first, last):
                for par in range(2):
                    sp.wait_ge(o_sent[par], 16 * last // 2)
                for g in range(2):
                    sp.dma_start(sh.o_raw[:, g, first:last, :], o_f[first:last, :, g * P:(g + 1) * P].rearrange("b d c -> d b c")).then_inc(sh.o_in[g], 16)

            for par in range(2):
                load_fresh(par, par, 0)
                load_fresh_v(par, par, 0)
            for g in range(2):
                sp.dma_start(sh.wo_raw[:, g, :, :], woT[g].rearrange("r p n -> p r n")).then_inc(sh.wo_in[g], 16)
            with sp.Fori(1, UNITS // TRIP) as trip:
                for par in range(2):
                    b, before = trip * 2 + par, trip * TRIP + (par - 1) * HK
                    page = page_numbers(nc, sh.table, b)
                    load_fresh(par, b, before)
                    load_pages(par, page)
                    load_fresh_v(par, b, before)
                    store(par, trip * 2 + (par - 2), before)
            load_heads(0, B - 2)
            for par in range(2):
                store(par, B - 2 + par, UNITS + (par - 1) * HK)
            load_heads(B - 2, B)

        @block.tensor
        def _(pe):
            def step(u):
                if u.within(UNITS):
                    p2, p4 = u.slot(2), u.slot(NS)
                    wait(pe, klo_done, u.n(1))
                    wait(pe, khi_done, u.n(1))
                    wait(pe, qlo_done, u.n(1))
                    wait(pe, max_done, u.n(-1))
                    for half in range(2):
                        ks = slice(half * HALF, (half + 1) * HALF)
                        out = SP_[p2][:, half, 0:HALF]
                        nc.tensor.matmul(out, q_hi[:, p4, :], k_hi[:, p4, ks], start=True, stop=False)
                        nc.tensor.matmul(out, q_hi[:, p4, :], k_lo[:, p4, ks], start=False, stop=False)
                        mm = nc.tensor.matmul(out, q_lo[:, p4, :], k_hi[:, p4, ks], start=False, stop=True)
                    mm.then_inc(s_done, 1)
                v = u.back(3)
                if v.within(UNITS):
                    wait(pe, pn_done, v.n(1))
                    wait(pe, pt_evac, v.n())
                    for c in range(4):
                        nc.tensor.transpose(TPa[:, c * P:(c + 1) * P], pn[:, v.slot(2), c * P:(c + 1) * P], ident[:, :])
                    nc.tensor.transpose(TPa[0:S, 4 * P:5 * P], pn[:, v.slot(2), CACHED:KEYS], ident[:, :]).then_inc(pt_done, 1)
                w = u.back(4)
                if w.within(UNITS):
                    par, h = (w.j // HK) % 2, w.j % HK
                    hd = slice(h * D, (h + 1) * D)
                    if h == 0:
                        wait(pe, v_in[par], trips(w) * (16 * VCH))
                        wait(pe, vf_in[par], trips(w) * 16)
                    wait(pe, pt_evac, w.n(1))
                    wait(pe, o_evac, w.n(-1))
                    out = OP[:, w.slot(2), 0:P]
                    for c in range(4):
                        nc.tensor.matmul(out, v_raw[:, par, c, hd], pT[:, w.slot(2), c * P:(c + 1) * P], start=(c == 0), stop=False)
                    nc.tensor.matmul(out, v_fresh[:, par, hd], pT[0:S, w.slot(2), 4 * P:5 * P], start=False, stop=True).then_inc(pv_done, 1)

            run(pe, step, 4)

        @block.scalar
        def _(act):
            def step(u):
                v = u.back(3)
                if v.within(UNITS):
                    wait(act, pt_done, v.n(1))
                    wait(act, pv_done, v.n(-1))
                    nc.scalar.copy(pT[:, v.slot(2), 0:4 * P], TPa[:, 0:4 * P])
                    nc.scalar.copy(pT[0:S, v.slot(2), 4 * P:5 * P], TPa[0:S, 4 * P:5 * P]).then_inc(pt_evac, 1)
                if u.within(UNITS):
                    wait(act, bias_done, u.n(1))
                    wait(act, pn_done, u.n(-3))
                    nc.scalar.activation(prob[:, u.slot(NS), :], score[:, u.slot(2), :], ACT.Exp,
                                         bias=nbias[:, u.slot(NS):u.slot(NS) + 1], scale=q_scale[:, bass.ds(u.n(), 1)],
                                         accum_out=total[:, u.slot(NS):u.slot(NS) + 1]).then_inc(exp_done, 1)
                w = u.back(4)
                if w.within(UNITS):
                    par, h = (w.j // HK) % 2, w.j % HK
                    if h == 0:
                        wait(act, o_sent[par], trips(w, 0) * 16)
                    wait(act, pv_done, w.n(1))
                    nc.scalar.copy(o_out[:, par, h * P:(h + 1) * P], OP[:, w.slot(2), 0:P]).then_inc(o_evac, 1)

            run(act, step, 4)

        @block.gpsimd
        def _(pool):
            def step(u):
                x = u.back(HK)
                if x.within(UNITS - HK) and x.j % HK < 3:
                    h, par = x.j % HK, (x.j // HK + 1) % 2
                    b = batch(x) + 1
                    if h == 0:
                        wait(pool, pv_done, x.n())
                        place_rows(nc, sh, b, par)
                    else:
                        waits(pool, pool_passed, [(sh.row_set, b + 1), (pv_done, x.n(-h))])
                        gather_values(nc, sh, v_c, par, range((h - 1) * VCH // 2, h * VCH // 2))
                if u.within(UNITS):
                    par, h, p4 = (u.j // HK) % 2, u.j % HK, u.slot(NS)
                    landed = [(k_in[par], trips(u) * (16 * NPG))] if h == 0 else []
                    waits(pool, pool_passed, landed + [(s_done, u.n(-3)), (klo_done, u.n(-3))])
                    nc.gpsimd.tensor_scalar(k_hi[:, p4, :].rearrange("p (n c) -> p n c", c=PSIZE),
                                            k_raw[:, par, :, h * PSIZE:(h + 1) * PSIZE], 1.0, 1.0, ALU.mult, ALU.mult).then_inc(khi_done, 1)
                v = u.back(4)
                if v.within(UNITS):
                    waits(pool, pool_passed, [(rec_done, v.n(1)), (pt_done, v.n(-1))])
                    nc.gpsimd.tensor_scalar(pn[:, v.slot(2), :], prob[:, v.slot(NS), :], rtotal[:, v.slot(NS):v.slot(NS) + 1], 1.0,
                                            ALU.mult, ALU.mult).then_inc(pn_done, 1)

            run(pool, step, 4)

        @block.vector
        def _(dve):
            dve.wait_ge(sh.attn_in, ATTN_IN)
            nc.vector.tensor_copy(seq_f[:, :], sh.seq_i[:, :]).then_inc(seq_cast, 1)
            nc.vector.memset(mask[:, :, CACHED:KEYS], 0.0).then_inc(mask_zero, 1)
            dve.wait_ge(seq_cast, 1)
            dve.wait_ge(mask_zero, 1)

            def step(u):
                if u.within(UNITS):
                    par, h, p4 = (u.j // HK) % 2, u.j % HK, u.slot(NS)
                    if h == 0:
                        wait(dve, q_in[par], trips(u) * 16)
                    wait(dve, s_done, u.n(-3))
                    nc.vector.tensor_copy(q_hi[:, p4, :], q_raw[:, par, h * P:(h + 1) * P]).then_inc(qhi_done, 1)
                    wait(dve, khi_done, u.n(1))
                    nc.vector.tensor_tensor(k_lo[:, p4, :].rearrange("p (n c) -> p n c", c=PSIZE),
                                            k_raw[:, par, :, h * PSIZE:(h + 1) * PSIZE],
                                            k_hi[:, p4, :].bitcast(F32).rearrange("p (n c) -> p n c", c=PSIZE), ALU.subtract).then_inc(klo_done, 1)
                    wait(dve, qhi_done, u.n(1))
                    nc.vector.tensor_tensor(q_lo[:, p4, :], q_raw[:, par, h * P:(h + 1) * P], q_hi[:, p4, :].bitcast(F32), ALU.subtract).then_inc(qlo_done, 1)
                v = u.back(2)
                if v.within(UNITS):
                    par, h, p4 = (v.j // HK) % 2, v.j % HK, v.slot(NS)
                    if h == 0:
                        wait(dve, max_done, v.n(-HK))
                        nc.vector.tensor_scalar(mask[:, par, 0:CACHED], sh.key[:, :], seq_f[:, bass.ds(batch(v), 1)], MASKED,
                                                ALU.is_ge, ALU.mult).then_inc(mask_done, 1)
                    masked = [(mask_done, batch(v) + 1)] if h == 0 else []
                    waits(dve, dve_passed, masked + [(s_done, v.n(1)), (exp_done, v.n(-1))])
                    nc.vector.tensor_tensor_reduce(score[:, v.slot(2), :].rearrange("p (a c) -> p a c", a=2), SP_[v.slot(2)][:, :, 0:HALF],
                                                   mask[:, par, :].rearrange("p (a c) -> p a c", a=2), 1.0, -3e38, ALU.add, ALU.max,
                                                   accum_out=top_s[:, p4:p4 + 1]).then_inc(max_done, 1)
                    wait(dve, max_done, v.n(1))
                    nc.vector.tensor_tensor(nbias[:, p4:p4 + 1], top_s[:, p4:p4 + 1], sh.q_nscale[:, bass.ds(v.n(), 1)], ALU.mult).then_inc(bias_done, 1)
                w = u.back(3)
                if w.within(UNITS):
                    p4 = w.slot(NS)
                    wait(dve, exp_done, w.n(1))
                    wait(dve, pn_done, w.n(-3))
                    nc.vector.reciprocal(rtotal[:, p4:p4 + 1], total[:, p4:p4 + 1]).then_inc(rec_done, 1)

            run(dve, step, 3)


def finish(nc, sh, x_tok, woT, cond, mix, o_f, out):
    s = Scope(nc)
    sb, sem = s.sb, s.sem
    with s.ctx:
        o_raw, w_raw, o_in, w_in = sh.o_raw, sh.wo_raw, sh.o_in, sh.wo_in
        o_hi = sb("o_hi", [P, 2, TOK], F32R)
        o_lo = sb("o_lo", [P, 2, TOK], F32R)
        w_hi = sb("wo_hi", [P, 2, HID], F32R)
        w_lo = sb("wo_lo", [P, 2, HID], F32R)
        x_sb = sb("x_sb", [P, TILES, HID])
        y_sb = sb("y_sb", [P, TILES, HID])
        cond_sb = sb("cond_sb", [1, B], I32)
        blocks = sb("blocks", [P, TILES, P])
        Y = [s.ps(f"Y{i}", [P, HID]) for i in range(TILES)]
        x_in, cond_in, zeroed, mix_in = sem("x_tok_in"), sem("cond_in"), sem("zeroed"), sem("mix_in")
        ohi_done, whi_done, parts_done, tile_done = sem("ohi_done"), sem("whi_done"), sem("parts_done"), sem("tile_done")
        res_done, mix_done, y_done, stored = sem("res_done"), sem("mixed"), sem("y_done"), sem("stored")

        def run(eng, step):
            for j in range(2 * R):
                step(Unit(0, j))
            with eng.Fori(1, HK // 2) as trip:
                for j in range(2 * R):
                    step(Unit(trip * (2 * R), j))

        block = s.ctx.enter_context(nc.Block())

        @block.sync
        def _(sp):
            def load(par, g, before):
                wait(sp, parts_done, before)
                sp.dma_start(o_raw[:, par, :, :], o_f[:, :, bass.ds(g * P, P)].rearrange("b d c -> d b c")).then_inc(o_in[par], 16)
                sp.dma_start(w_raw[:, par, :, :], woT[bass.ds(g, 1)].rearrange("o r p n -> p (o r) n")).then_inc(w_in[par], 16)
            sp.dma_start(cond_sb[:, :], cond).then_inc(cond_in, 16)
            sp.dma_start(x_sb[:, :, :], x_tok.rearrange("(t p) n -> p t n", p=P)).then_inc(x_in, 16)
            sp.wait_ge(cond_in, 16)
            sp.wait_ge(zeroed, 1)
            for b in range(B):
                c = sp.value_load(cond_sb[0:1, b:b + 1], min_val=0, max_val=15)
                q = (b % BT) * S
                sp.dma_start(blocks[q:q + S, b // BT, q:q + S], mix[bass.ds(c, 1)].rearrange("o c d -> c (o d)")).then_inc(mix_in, 16)
            with sp.Fori(1, HK // 2) as trip:
                for par in range(2):
                    load(par, trip * 2 + par, trip * (2 * R) + (par - 1) * R)
            o_tiles = out.rearrange("(t p) n -> t p n", p=P)
            for t in range(TILES):
                sp.wait_ge(y_done, t + 1)
                sp.dma_start(o_tiles[t], y_sb[:, t, :]).then_inc(stored, 16)
            sp.wait_ge(stored, 16 * TILES)

        @block.gpsimd
        def _(pool):
            nc.gpsimd.memset(blocks[:, :, :], 0.0).then_inc(zeroed, 1)

        @block.vector
        def _(dve):
            def step(u):
                par, r, p2 = (u.j // R) % 2, u.j % R, u.slot(2)
                if r == 0:
                    wait(dve, o_in[par], (u.base // (2 * R)) * 16 + 32)
                    wait(dve, w_in[par], (u.base // (2 * R)) * 16 + 16)
                wait(dve, tile_done, u.n(-1) * TILES)
                src = o_raw[:, par, :, r * S:(r + 1) * S]
                nc.vector.tensor_copy(w_hi[:, p2, :], w_raw[:, par, r, :]).then_inc(whi_done, 1)
                nc.vector.tensor_copy(o_hi[:, p2, :].rearrange("p (b s) -> p b s", s=S), src).then_inc(ohi_done, 1)
                wait(dve, whi_done, u.n(1))
                nc.vector.tensor_tensor(w_lo[:, p2, :], w_raw[:, par, r, :], w_hi[:, p2, :].bitcast(F32), ALU.subtract)
                wait(dve, ohi_done, u.n(1))
                nc.vector.tensor_tensor(o_lo[:, p2, :].rearrange("p (b s) -> p b s", s=S), src,
                                        o_hi[:, p2, :].bitcast(F32).rearrange("p (b s) -> p b s", s=S), ALU.subtract).then_inc(parts_done, 1)

            run(dve, step)
            dve.wait_ge(x_in, 16)
            for t in range(TILES + 2):
                if t < TILES:
                    dve.wait_ge(tile_done, (HQ - 1) * TILES + t + 1)
                    nc.vector.tensor_tensor(x_sb[:, t, :], x_sb[:, t, :], Y[t][:, :], ALU.add).then_inc(res_done, 1)
                if t >= 2:
                    dve.wait_ge(mix_done, t - 1)
                    nc.vector.tensor_tensor(y_sb[:, t - 2, :], x_sb[:, t - 2, :], Y[t - 2][:, :], ALU.add).then_inc(y_done, 1)

        @block.tensor
        def _(pe):
            def step(u):
                p2 = u.slot(2)
                first = u.static() and u.n() == 0
                wait(pe, parts_done, u.n(1))
                for t in range(TILES):
                    cols = slice(t * P, (t + 1) * P)
                    nc.tensor.matmul(Y[t][:, :], o_hi[:, p2, cols], w_hi[:, p2, :], start=first, stop=False, skip_group_check=True)
                    nc.tensor.matmul(Y[t][:, :], o_hi[:, p2, cols], w_lo[:, p2, :], start=False, stop=False, skip_group_check=True)
                    nc.tensor.matmul(Y[t][:, :], o_lo[:, p2, cols], w_hi[:, p2, :], start=False, stop=True, skip_group_check=True).then_inc(tile_done, 1)

            run(pe, step)
            pe.wait_ge(mix_in, 16 * B)
            for t in range(TILES):
                pe.wait_ge(res_done, t + 1)
                nc.tensor.matmul(Y[t][:, :], blocks[:, t, :], x_sb[:, t, :], start=True, stop=True).then_inc(mix_done, 1)


def program(nc, xT, x_tok, w_all, woT, seq, seq_tile, pages, page_of_chunk, cond, q_w, k_w, kT, v_c, mix, inv_freq, sidx, iota, eye, out):
    kq_f = nc.dram_tensor("kq_fresh", [B, D, HK * S + HK * P], F32).ap()
    v_f = nc.dram_tensor("v_fresh_all", [B, S, HK * D], F32).ap()
    o_f = nc.dram_tensor("heads_out", [B, D, HK * P], F32).ap()
    sh = Shared(nc)
    with sh.ctx:
        project(nc, sh, xT, w_all, seq_tile, seq, inv_freq, sidx, q_w, k_w, pages, page_of_chunk, kT, v_c, iota, eye, kq_f, v_f.rearrange("b s c -> (b s) c"))
        attend(nc, sh, kT, v_c, kq_f, v_f, o_f, woT)
        finish(nc, sh, x_tok, woT, cond, mix, o_f, out)


def kernel(**inputs):
    import concourse.bacc as _bacc
    from concourse.bass_utils import run_bass_kernel_spmd as _run

    a = {k: np.asarray(v) for k, v in inputs.items()}
    cont = np.ascontiguousarray
    x = a["x"].reshape(TOK, HID)
    w_all = np.concatenate([a["L0_cond_Wv"], a["L0_cond_Wk"], a["L0_cond_Wq"]], axis=0)
    half = np.arange(0, D, 2, dtype=np.float32) / np.float32(D)
    arrays = {
        "xT": cont(x.T.reshape(KC, P, TOK).transpose(1, 0, 2)),
        "x_tok": cont(x),
        "w_all": cont(w_all.reshape(CHUNKS, NC_, KC, P).transpose(0, 3, 2, 1)),
        "woT": cont(a["L0_cond_Wo"].T.reshape(HK, R, P, HID)),
        "seq": cont(a["itok_B_207_1644"]),
        "seq_tile": cont(a["itok_B_207_1644"].reshape(TILES, BT).T.reshape(-1)),
        "pages": cont(a["itok_Bx16_0_63"].reshape(1, B * NPP)),
        "page_of_chunk": cont(a["itok_Bx16_0_63"].reshape(B * VCH, BT).T),
        "cond": cont(a["itok_B_0_15"].reshape(1, B)),
        "q_w": cont(a["L0_cond_q_norm_w"]),
        "k_w": cont(a["L0_cond_k_norm_w"]),
        "kT": cont(a["L0_cond_k_cache"].transpose(0, 3, 2, 1).reshape(PAGES, D, HK * PSIZE)),
        "v_c": cont(a["L0_cond_v_cache"].reshape(PAGES * PSIZE, HK * D)),
        "mix": cont(a["L1_cond_weights"]),
        "inv_freq": (np.float32(1) / (10000.0 ** half.astype(np.float64)).astype(np.float32)).astype(np.float32),
        "sidx": (np.arange(P) % S).astype(np.float32).reshape(P, 1),
        "iota": np.arange(CACHED).astype(np.float32),
        "eye": np.eye(P, dtype=np.float32),
    }
    nc = _bacc.Bacc("TRN2", target_bir_lowering=False, num_devices=1)
    args = [nc.dram_tensor(f"in_{k}", v.shape, mybir.dt.from_np(v.dtype), kind="ExternalInput").ap() for k, v in arrays.items()]
    out = nc.dram_tensor("out_y", [TOK, HID], F32, kind="ExternalOutput").ap()
    program(nc, *args, out)
    r = _run(nc, [{f"in_{k}": v for k, v in arrays.items()}], core_ids=[0])
    return r.results[0]["out_y"].reshape(B, S, HID)
```

```python
from contextlib import ExitStack

import numpy as np
import concourse.bass as bass
from concourse import mybir

F32 = mybir.dt.float32
F32R = mybir.dt.float32r
I32 = mybir.dt.int32
ALU = mybir.AluOpType
ACT = mybir.ActivationFunctionType
AX = mybir.AxisListType

P = 128
B, S, HID = 32, 32, 512
D, HQ, HK = 128, 32, 8
R = HQ // HK
PAGES, PSIZE, NPP = 64, 32, 16
CACHED = NPP * PSIZE
KEYS = CACHED + S
HALF = KEYS // 2
NPG = NPP + 1
PLACES = NPP + 2
TOK = B * S
TILES = TOK // P
BT = P // S
KC = HID // P
NC_ = 512
CHUNKS = 2 * HK * D // NC_ + HQ * D // NC_
EPS = 1e-6
SCALE = 1.0 / float(np.sqrt(D))
MASKED = -1e30
UNITS = B * HK
KEPT = 2
HI_AT = (1, 3, 4, 5)
LO_AT = (2, 4, 5, 6)
GATHER_LAG = 6
GATHER_AT = (1, 3, 5, 6)
ATTN_IN = 16 * (3 + BT)
VCH = CACHED // P
TRIP = 16
MAGIC = 1.5 * 2.0 ** 23
PI2_A = 6.28125
PI2_B = float(np.float32(np.floor((2 * np.pi - PI2_A) * 2.0 ** 20) / 2.0 ** 20))
PI2_C = float(np.float32(2 * np.pi - PI2_A - PI2_B))


class Unit:

    def __init__(self, base, j):
        self.base, self.j = base, j

    def back(self, n):
        return Unit(self.base, self.j - n)

    def n(self, plus=0):
        return self.base + (self.j + plus)

    def static(self):
        return isinstance(self.base, int)

    def within(self, end):
        return not self.static() or 0 <= self.n() < end

    def slot(self, k):
        return self.j % k


def wait(eng, sem, value):
    if not isinstance(value, int) or value > 0:
        eng.wait_ge(sem, value)


def waits(eng, passed, pairs):
    for sem, v in pairs:
        wait(eng, sem, v)
    eng.sem_inc(passed, 1)


class Scope:
    def __init__(self, nc):
        self.nc, self.ctx = nc, ExitStack()

    def sb(self, name, shape, dt=F32):
        return self.ctx.enter_context(self.nc.sbuf_tensor(name, shape, dt))

    def ps(self, name, shape, dt=F32):
        return self.ctx.enter_context(self.nc.psum_tensor(name, shape, dt))

    def sem(self, name):
        return self.ctx.enter_context(self.nc.semaphore(name))


class Late(Scope):

    def __init__(self, nc):
        super().__init__(nc)
        self.o_out = self.sb("o_out", [P, 2, (HK - KEPT) * P])
        self.o_hi = self.sb("o_hi_even", [P, TOK], F32R)
        self.o_lo = self.sb("o_lo_even", [P, TOK], F32R)
        self.w_hi = self.sb("wo_hi_even", [P, HID], F32R)
        self.w_lo = self.sb("wo_lo_even", [P, HID], F32R)


class Shared(Scope):

    def __init__(self, nc):
        super().__init__(nc)
        sb, sem = self.sb, self.sem
        self.ident = sb("ident", [P, P])
        self.q_scale = sb("q_scale", [P, UNITS])
        self.q_nscale = sb("q_nscale", [P, UNITS])
        self.table = sb("table", [1, B * NPP], I32)
        self.page_i = sb("page_i", [P, B * VCH], I32)
        self.slot_of_p = sb("slot_of_p", [P, 1])
        self.v_row = sb("v_row", [P, B * VCH], I32)
        self.row_now = sb("row_now", [P, 2, VCH], I32)
        self.seq_i = sb("seq_i", [P, B], I32)
        self.key = sb("key", [P, CACHED])
        self.q_rs = sb("q_rs", [P, TILES, HQ])
        self.q_raw = sb("q_raw", [P, 2, HK * P])
        self.v_fresh = sb("v_fresh", [2 * S, 2, HK // 2, D])
        self.k_raw = sb("k_raw", [P, 2, PLACES, HK * PSIZE])
        self.v_raw = sb("v_raw", [P, 2, VCH, HK * D])
        self.o_raw = sb("o_raw", [P, 2, B, R * S])
        self.wo_raw = sb("wo_raw", [P, 2, R, HID])
        self.attn_in, self.rows_done, self.row_set = sem("attn_in"), sem("rows_done"), sem("row_set")
        self.k_in = [sem("k_in0"), sem("k_in1")]
        self.v_in = [sem("v_in0"), sem("v_in1")]
        self.q_in = [sem("q_in0"), sem("q_in1")]
        self.vf_in = [sem("vf_in0"), sem("vf_in1")]
        self.kqv_sent = [sem(f"kqv_sent{i}") for i in range(4)]
        self.o_sent = [sem("o_sent0"), sem("o_sent1")]
        self.o_in = [sem("o_in0"), sem("o_in1")]
        self.wo_in = [sem("wo_in0"), sem("wo_in1")]


def page_numbers(nc, table, b):
    return nc.values_load_multi_w_load_instructions(table[0:1, bass.ds(b * NPP, NPP)], engines=(mybir.EngineType.SP,),
                                                    min_val=0, max_val=PAGES - 1,
                                                    skip_runtime_bounds_check_because="a page number is below PAGES, and the DMA that uses it is checked")[1]


def gather_values(nc, sh, v_c, par, chunks):
    for c in chunks:
        nc.gpsimd.indirect_dma_start(sh.v_raw[:, par, c, :], None, v_c, bass.IndirectOffsetOnAxis(sh.row_now[:, par, c:c + 1], 0),
                                     bounds_check=PAGES * PSIZE - 1).then_inc(sh.v_in[par], 16)


def place_rows(nc, sh, b, par):
    nc.gpsimd.tensor_copy(sh.row_now[:, par, :], sh.v_row[:, bass.ds(b * VCH, VCH)]).then_inc(sh.row_set, 1)


def load_fresh(nc, sh, kq_f, par, b):
    nc.sync.dma_start(sh.q_raw[:, par, :], kq_f[bass.ds(b, 1), :, HK * S:].rearrange("o d c -> d (o c)")).then_inc(sh.q_in[par], 16)
    for place in (0, PLACES - 1):
        nc.sync.dma_start(sh.k_raw[:, par, place, :], kq_f[bass.ds(b, 1), :, 0:HK * S].rearrange("o d c -> d (o c)")).then_inc(sh.k_in[par], 16)


def load_fresh_v(nc, sh, v_f, par, b):
    src = v_f[bass.ds(b, 1)].rearrange("o s (k e d) -> s e (o k) d", e=2, d=D)
    for odd in range(2):
        nc.sync.dma_start(sh.v_fresh[odd * S:(odd + 1) * S, par, :, :], src[:, odd, :, :]).then_inc(sh.vf_in[par], 16)


def heads4(ap):
    return ap.rearrange("p (h d) -> p h d", d=D)


def project(nc, sh, xT, w_all, seq_tile, seq, inv_freq, sidx, q_w, k_w, pages, page_of_chunk, kT, v_c, iota, ident_d, kq_f, v_f):
    s = Scope(nc)
    sb, sem = s.sb, s.sem
    with s.ctx:
        def part(buf, at, n, shape, names):
            dims = dict(zip(names[:-1], shape))
            flat = buf.rearrange("p a b -> p (a b)")[:, at:at + n]
            return flat.rearrange("p (%s) -> p %s" % (" ".join(names), " ".join(names)), **dims)

        k0, k1, v1 = sh.k_raw[:, 0, :, :], sh.k_raw[:, 1, :, :], sh.v_raw[:, 1, :, :]
        spare = sh.o_raw[:, :, :, :].rearrange("p a b c -> p a (b c)")
        TD, TH = TILES * D, TILES * D // 2
        x_raw = part(k0, 0, KC * TOK, [KC], "kt")
        ident = sh.ident
        x_hi = sb("x_hi", [P, KC, TOK], F32R)
        x_lo = sb("x_lo", [P, KC, TOK], F32R)
        w_raw = sh.wo_raw
        w_hi = sb("w_hi", [P, 2, KC, NC_], F32R)
        w_lo = sb("w_lo", [P, 2, KC, NC_], F32R)
        pos_i = sb("pos_i", [P, TILES], I32)
        pos_f = sb("pos_f", [P, TILES])
        inv = sb("inv", [P, D // 2])
        wb = sb("wb", [P, 2, D])
        ang = part(k1, 0, TH, [TILES], "td")
        turn = part(k1, TH, TH, [TILES], "td")
        sin_t = part(k1, 2 * TH, TH, [TILES], "td")
        cos_t = part(k1, 3 * TH, TH, [TILES], "td")
        rope_c = part(v1, 0, 2 * TD, [2, TILES], "qtd")
        rope_s = part(v1, 2 * TD, 2 * TD, [2, TILES], "qtd")
        sq = part(spare, 0, 2 * NC_, [2], "sn")
        raw = part(spare, 2 * NC_, 2 * NC_, [2], "sn")
        m1 = part(spare, 4 * NC_, 2 * NC_, [2], "sn")
        m2 = part(spare, 6 * NC_, 2 * NC_, [2], "sn")
        rp = part(spare, 8 * NC_, 4 * NC_, [4], "sn")
        outb = part(spare, 12 * NC_, 4 * NC_, [4], "sn")
        page_f = sb("page_f", [P, B * VCH])
        ss = sb("ss", [P, 2, 4])
        ms = sb("ms", [P, 2, 4])
        k_rs = sb("k_rs", [P, 2, 4])
        q_rs = sh.q_rs
        minus_half = sb("minus_half", [P, 4])
        QP = [s.ps(f"QP{i}", [P, NC_]) for i in range(4)]
        TP = [s.ps(f"TP{i}", [P, NC_]) for i in range(4)]

        x_in, w0_in = [sem(f"x_in{k}") for k in range(KC)], [sem(f"w0_in{k}") for k in range(KC)]
        small_in, ident_in, page_cast = sem("small_in"), sem("ident_in"), sem("page_cast")
        w_in = [sem("w_in0"), sem("w_in1")]
        x_hi_done, x_split = sem("x_hi_done"), sem("x_split")
        w0_hi_done, w0_split = sem("w0_hi_done"), sem("w0_split")
        w_hi_done, w_split = sem("w_hi_done"), sem("w_split")
        tab, trig = sem("tab"), sem("trig")
        mm_done, qp_read, m1_done = sem("mm_done"), sem("qp_read"), sem("m1_done")
        sq_done = sem("sq_done")
        ss_done, ms_done, rs_done = sem("ss_done"), sem("ms_done"), sem("rs_done")
        m2_done, add_done, rp_done = sem("m2_done"), sem("add_done"), sem("rp_done")
        t_done, t_evac = sem("t_done"), sem("t_evac")
        out_sent = sh.kqv_sent
        const_set, table_step = sem("const_set"), sem("table_step")

        KU = 2 * TILES
        NU = CHUNKS * TILES

        def kind(u):
            if not u.static():
                return "q"
            return "v" if u.n() < KU else "k" if u.n() < 2 * KU else "q"

        def turned(u):
            return u.n(-KU)

        def run(eng, step, lag):
            pairs = NU // TRIP
            for pair in range(2):
                for j in range(TRIP):
                    step(Unit(pair * TRIP, j))
            with eng.Fori(2, pairs - 1) as pair:
                for j in range(TRIP):
                    step(Unit(pair * TRIP, j))
            for j in range(TRIP + lag):
                step(Unit((pairs - 1) * TRIP, j))

        block = s.ctx.enter_context(nc.Block())

        @block.sync
        def _(sp):
            for k in range(KC):
                sp.dma_start(x_raw[:, k, :], xT[:, k, :]).then_inc(x_in[k], 16)
                sp.dma_start(w_raw[:, 0, k, :], w_all[0][:, k, :]).then_inc(w0_in[k], 16)
            for bl in range(BT):
                src = seq_tile[bl * TILES:(bl + 1) * TILES].partition_broadcast(S)
                sp.dma_start(pos_i[bl * S:(bl + 1) * S, :], src).then_inc(small_in, 16)
            sp.dma_start(sh.slot_of_p[:, :], sidx).then_inc(small_in, 16)
            sp.dma_start(inv[:, :], inv_freq.partition_broadcast(P)).then_inc(small_in, 16)
            sp.dma_start(wb[:, 0, :], q_w.partition_broadcast(P)).then_inc(small_in, 16)
            sp.dma_start(wb[:, 1, :], k_w.partition_broadcast(P)).then_inc(small_in, 16)
            sp.dma_start(ident[:, :], ident_d).then_inc(ident_in, 16)
            sp.dma_start(w_raw[:, 1, :, :], w_all[1]).then_inc(w_in[1], 16)
            for g in range(BT):
                sp.dma_start(sh.page_i[g * PSIZE:(g + 1) * PSIZE, :], page_of_chunk[g].partition_broadcast(PSIZE)).then_inc(sh.attn_in, 16)
            sp.dma_start(sh.table[:, :], pages).then_inc(sh.attn_in, 16)
            sp.dma_start(sh.seq_i[:, :], seq.partition_broadcast(P)).then_inc(sh.attn_in, 16)
            sp.dma_start(sh.key[:, :], iota.partition_broadcast(P)).then_inc(sh.attn_in, 16)
            early_page = [None] * NPP

            def early_pages(u):
                b, n = (u.n() - TRIP) // 8, u.j % 8 * 2
                if n == 0:
                    if b == 0:
                        sp.wait_ge(sh.attn_in, ATTN_IN)
                        sp.wait_ge(x_split, KC)
                    else:
                        sp.wait_ge(tab, 2)
                    early_page[:] = page_numbers(nc, sh.table, b)
                for i in (n, n + 1):
                    sp.dma_start(sh.k_raw[:, b, 1 + i, :], kT[bass.ds(early_page[i], 1)].rearrange("o d c -> d (o c)")).then_inc(sh.k_in[b], 16)

            def step(u):
                if u.static() and TRIP <= u.n() < 2 * TRIP:
                    early_pages(u)
                if u.slot(TILES) == 2 and (not u.static() or u.n() // TILES + 2 < CHUNKS):
                    chunk = Unit(u.base // TILES, u.j // TILES)
                    slot = (u.j // TILES) % 2
                    if chunk.static() and chunk.n() == 0:
                        sp.wait_ge(w0_split, KC)
                    wait(sp, w_split, chunk.n())
                    sp.dma_start(w_raw[:, slot, :, :], w_all[bass.ds(chunk.n(2), 1)].rearrange("o p k n -> p (o k) n")).then_inc(w_in[slot], 16)
                v = u.back(2)
                if not v.within(NU):
                    return
                o = v.slot(4)
                wait(sp, t_evac, v.n(1))
                tile = v.j % TILES
                if kind(v) == "v":
                    chunk = v.n() // TILES
                    dst = v_f[tile * P:(tile + 1) * P, chunk * NC_:(chunk + 1) * NC_]
                    src = outb[:, o, :]
                else:
                    col = (v.base // TILES + (v.j // TILES - 2)) * P
                    dst = kq_f[tile * BT:(tile + 1) * BT, :, bass.ds(col, P)].rearrange("b d c -> d b c")
                    src = outb[:, o, :].rearrange("p (b c) -> p b c", b=BT)
                sp.dma_start(dst, src).then_inc(out_sent[o], 16)
                if v.static() and v.n() == NU - TILES + 3:
                    sp.wait_ge(out_sent[0], 16 * ((NU - TILES) // 4 + 1))
                    for b in range(2):
                        load_fresh(nc, sh, kq_f, b, b)
                        load_fresh_v(nc, sh, v_f.rearrange("(b s) c -> b s c", s=S), b, b)

            run(sp, step, 2)

        @block.tensor
        def _(pe):
            for k in range(KC):
                def products(x, w, **flags):
                    for t in range(4):
                        mm = nc.tensor.matmul(QP[t][:, :], x[:, k, t * P:(t + 1) * P], w[:, 0, k, :], **flags)
                        if flags["stop"]:
                            mm.then_inc(mm_done, 1)
                pe.wait_ge(x_hi_done, k + 1)
                pe.wait_ge(w0_hi_done, k + 1)
                products(x_hi, w_hi, start=k == 0, stop=False)
                pe.wait_ge(x_split, k + 1)
                products(x_lo, w_hi, start=False, stop=False)
                pe.wait_ge(w0_split, k + 1)
                products(x_hi, w_lo, start=False, stop=k == KC - 1)

            def step(u):
                if u.within(NU) and not (u.static() and u.n() < 4):
                    if u.slot(TILES) == 0:
                        wait(pe, w_split, u.base // TILES + u.j // TILES)
                    wait(pe, qp_read, u.n(-3))
                    tile, slot = u.j % TILES, (u.j // TILES) % 2
                    cols = slice(tile * P, (tile + 1) * P)
                    bank = QP[u.slot(4)]
                    for k in range(KC):
                        nc.tensor.matmul(bank[:, :], x_hi[:, k, cols], w_hi[:, slot, k, :], start=(k == 0), stop=False)
                        nc.tensor.matmul(bank[:, :], x_hi[:, k, cols], w_lo[:, slot, k, :], start=False, stop=False)
                        mm = nc.tensor.matmul(bank[:, :], x_lo[:, k, cols], w_hi[:, slot, k, :], start=False, stop=(k == KC - 1))
                    mm.then_inc(mm_done, 1)
                v = u.back(2)
                if v.within(NU) and kind(v) != "v":
                    if v.static() and v.n() == KU:
                        pe.wait_ge(ident_in, 16)
                    wait(pe, rp_done, turned(v) + 1)
                    wait(pe, t_evac, v.n(-3))
                    for h in range(4):
                        tr = nc.tensor.transpose(TP[v.slot(4)][:, h * P:(h + 1) * P], rp[:, v.slot(4), h * D:(h + 1) * D], ident[:, :])
                    tr.then_inc(t_done, 1)

            run(pe, step, 2)

        @block.scalar
        def _(act):
            for k in range(KC):
                act.wait_ge(x_in[k], 16)
                nc.scalar.copy(x_hi[:, k, :], x_raw[:, k, :]).then_inc(x_hi_done, 1)
                act.wait_ge(w0_in[k], 16)
                nc.scalar.copy(w_hi[:, 0, k, :], w_raw[:, 0, k, :]).then_inc(w0_hi_done, 1)

            def step(u):
                if u.static() and u.n() == 7:
                    act.wait_ge(tab, 1)
                    nc.scalar.activation(sin_t, sin_t, ACT.Sin).then_inc(trig, 1)
                    nc.scalar.activation(cos_t, cos_t, ACT.Sin).then_inc(trig, 1)
                if u.within(NU):
                    bank = QP[u.slot(4)]
                    wait(act, mm_done, u.n(1))
                    if kind(u) == "v":
                        o = u.slot(4)
                        wait(act, out_sent[o], u.n(-o) * 4)
                        nc.scalar.copy(outb[:, o, :], bank[:, :]).then_inc(qp_read, 1)
                    else:
                        wait(act, ss_done, turned(u) - 1)
                        nc.scalar.activation(sq[:, u.slot(2), :], bank[:, :], ACT.Square).then_inc(sq_done, 1)
                        wait(act, m1_done, turned(u) - 1)
                        wait(act, m2_done, turned(u) - 1)
                        nc.scalar.copy(raw[:, u.slot(2), :], bank[:, :]).then_inc(qp_read, 1)
                v = u.back(2)
                if v.within(NU):
                    if kind(v) == "v":
                        wait(act, qp_read, v.n(1))
                        act.sem_inc(t_evac, 1)
                    else:
                        o = v.slot(4)
                        wait(act, t_done, turned(v) + 1)
                        wait(act, out_sent[o], v.n(-o) * 4)
                        dst = outb[:, o, :].rearrange("p (b r s) -> p r b s", b=BT, r=4)
                        src = TP[v.slot(4)][:, :].rearrange("p (r b s) -> p r b s", b=BT, r=4)
                        nc.scalar.copy(dst, src).then_inc(t_evac, 1)
                nxt, tile = Unit(u.base // TILES, u.j // TILES + 1), u.j % TILES
                if tile in HI_AT and (not nxt.static() or nxt.n() < CHUNKS):
                    slot, k = nxt.j % 2, HI_AT.index(tile)
                    if k == 0:
                        wait(act, w_in[slot], (nxt.base // 2 + (nxt.j // 2 + slot)) * 16)
                    nc.scalar.copy(w_hi[:, slot, k, :], w_raw[:, slot, k, :]).then_inc(w_hi_done, 1)

            run(act, step, 2)

        @block.gpsimd
        def _(pool):
            nc.gpsimd.memset(minus_half[:, :], -0.5).then_inc(const_set, 1)
            pool.wait_ge(const_set, 1)

            def step(u):
                if kind(u) == "v":
                    return
                n, p2, qk = turned(u), u.slot(2), int(kind(u) == "k")
                tile = u.j % TILES
                wait(pool, qp_read, u.n(1))
                wait(pool, rp_done, n - 1)
                r, o = heads4(raw[:, p2, :]), heads4(m2[:, p2, :])
                for half in range(2):
                    a, c = half * 64, (1 - half) * 64
                    tt = nc.gpsimd.tensor_tensor(o[:, :, a:a + 64], r[:, :, c:c + 64],
                                                 rope_s[:, qk, tile:tile + 1, a:a + 64].to_broadcast([P, 4, 64]), ALU.mult)
                tt.then_inc(m2_done, 1)
                wait(pool, ms_done, n + 1)
                if qk:
                    rs = k_rs[:, p2, :]
                else:
                    rs = q_rs[:, tile, bass.ds((u.base // TILES + (u.j // TILES - 4)) * 4, 4)]
                nc.gpsimd.tensor_tensor(rs, ms[:, p2, :], minus_half[:, :], ALU.pow).then_inc(rs_done, 1)

            pool.wait_ge(sh.rows_done, 1)
            place_rows(nc, sh, 0, 0)
            pool.wait_ge(sh.row_set, 1)
            pool.wait_ge(tab, 2)
            gather_values(nc, sh, v_c, 0, range(VCH))
            run(pool, step, 0)

        @block.vector
        def _(dve):
            link = [0]

            def then(ins):
                link[0] += 1
                ins.then_inc(table_step, 1)
                dve.wait_ge(table_step, link[0])

            for k in range(KC):
                dve.wait_ge(x_hi_done, k + 1)
                nc.vector.tensor_tensor(x_lo[:, k, :], x_raw[:, k, :], x_hi[:, k, :].bitcast(F32), ALU.subtract).then_inc(x_split, 1)
                dve.wait_ge(w0_hi_done, k + 1)
                nc.vector.tensor_tensor(w_lo[:, 0, k, :], w_raw[:, 0, k, :], w_hi[:, 0, k, :].bitcast(F32), ALU.subtract).then_inc(w0_split, 1)
            dve.wait_ge(small_in, 16 * (BT + 4))
            then(nc.vector.tensor_copy(pos_f[:, :], pos_i[:, :]))
            then(nc.vector.tensor_scalar(pos_f[:, :], pos_f[:, :], sh.slot_of_p[:, :], None, ALU.add))
            then(nc.vector.tensor_tensor(ang[:, :, :], pos_f[:, :].unsqueeze(2).to_broadcast([P, TILES, D // 2]),
                                         inv[:, :].unsqueeze(1).to_broadcast([P, TILES, D // 2]), ALU.mult))
            for t, off in ((sin_t, 0.0), (cos_t, 0.25)):
                then(nc.vector.tensor_scalar(turn[:, :, :], ang[:, :, :], 1 / (2 * np.pi), off, ALU.mult, ALU.add))
                then(nc.vector.tensor_scalar(turn[:, :, :], turn[:, :, :], MAGIC, MAGIC, ALU.add, ALU.subtract))
                then(nc.vector.scalar_tensor_tensor(t[:, :, :], turn[:, :, :], -PI2_A, ang[:, :, :], ALU.mult, ALU.add))
                then(nc.vector.scalar_tensor_tensor(t[:, :, :], turn[:, :, :], -PI2_B, t[:, :, :], ALU.mult, ALU.add))
                then(nc.vector.scalar_tensor_tensor(t[:, :, :], turn[:, :, :], -PI2_C, t[:, :, :], ALU.mult, ALU.add))
                if off:
                    then(nc.vector.tensor_scalar(t[:, :, :], t[:, :, :], float(np.pi / 2), None, ALU.add))
                then(nc.vector.tensor_scalar(t[:, :, :], t[:, :, :], 3.1415925, -3.1415925, ALU.min, ALU.max))
            nc.vector.memset(ms[:, :, :], 0.0).then_inc(tab, 1)
            dve.wait_ge(sh.attn_in, ATTN_IN)
            nc.vector.tensor_scalar(page_f[:, :], sh.page_i[:, :], float(PSIZE), sh.slot_of_p[:, :], ALU.mult, ALU.add).then_inc(page_cast, 1)
            dve.wait_ge(page_cast, 1)
            nc.vector.tensor_copy(sh.v_row[:, :], page_f[:, :]).then_inc(sh.rows_done, 1)

            def rope_tables():
                dve.wait_ge(trig, 2)
                for qk in range(2):
                    w1 = wb[:, qk:qk + 1, 0:64].to_broadcast([P, TILES, 64])
                    w2 = wb[:, qk:qk + 1, 64:128].to_broadcast([P, TILES, 64])
                    nc.vector.tensor_tensor(rope_c[:, qk, :, 0:64], cos_t[:, :, :], w1, ALU.mult)
                    nc.vector.tensor_tensor(rope_c[:, qk, :, 64:128], cos_t[:, :, :], w2, ALU.mult)
                    nc.vector.scalar_tensor_tensor(rope_s[:, qk, :, 0:64], sin_t[:, :, :], -1.0, w2, ALU.mult, ALU.mult)
                    last = nc.vector.tensor_tensor(rope_s[:, qk, :, 64:128], sin_t[:, :, :], w1, ALU.mult)
                last.then_inc(tab, 1)
                dve.wait_ge(tab, 2)

            def step(u):
                if u.static() and u.n() == 9:
                    rope_tables()
                p2, tile = u.slot(2), u.j % TILES
                nxt = Unit(u.base // TILES, u.j // TILES + 1)
                if tile in LO_AT and (not nxt.static() or nxt.n() < CHUNKS):
                    slot, k = nxt.j % 2, LO_AT.index(tile)
                    wait(dve, w_hi_done, nxt.n(-1) * KC + (k + 1))
                    ins = nc.vector.tensor_tensor(w_lo[:, slot, k, :], w_raw[:, slot, k, :], w_hi[:, slot, k, :].bitcast(F32), ALU.subtract)
                    if k == KC - 1:
                        ins.then_inc(w_split, 1)
                if kind(u) == "v":
                    return
                n, qk = turned(u), int(kind(u) == "k")
                wait(dve, sq_done, n + 1)
                wait(dve, rs_done, n - 1)
                nc.vector.reduce_sum(ss[:, p2, :], heads4(sq[:, p2, :]), AX.X).then_inc(ss_done, 1)
                wait(dve, ss_done, n + 1)
                nc.vector.tensor_scalar(ms[:, p2, :], ss[:, p2, :], 1.0 / D, EPS, ALU.mult, ALU.add).then_inc(ms_done, 1)
                wait(dve, qp_read, u.n(1))
                wait(dve, rp_done, n - 1)
                nc.vector.tensor_tensor(heads4(m1[:, p2, :]), heads4(raw[:, p2, :]),
                                        rope_c[:, qk, tile:tile + 1, :].to_broadcast([P, 4, D]), ALU.mult).then_inc(m1_done, 1)
                wait(dve, m2_done, n + 1)
                wait(dve, m1_done, n + 1)
                wait(dve, t_done, n - 3)
                if qk:
                    nc.vector.tensor_tensor(m1[:, p2, :], m1[:, p2, :], m2[:, p2, :], ALU.add).then_inc(add_done, 1)
                    wait(dve, add_done, n + 1)
                    wait(dve, rs_done, n + 1)
                    nc.vector.tensor_tensor(heads4(rp[:, u.slot(4), :]), heads4(m1[:, p2, :]),
                                            k_rs[:, p2, :].unsqueeze(2).to_broadcast([P, 4, D]), ALU.mult).then_inc(rp_done, 1)
                else:
                    nc.vector.tensor_tensor(rp[:, u.slot(4), :], m1[:, p2, :], m2[:, p2, :], ALU.add).then_inc(rp_done, 1)

            run(dve, step, 0)


def attend(nc, sh, late, kT, v_c, kq_f, v_f, o_f, woT):
    s = Scope(nc)
    sb, sem = s.sb, s.sem
    with s.ctx:
        NS = 4
        k_raw, v_raw, ident, q_scale = sh.k_raw, sh.v_raw, sh.ident, sh.q_scale
        k_in, v_in = sh.k_in, sh.v_in
        v_fresh, q_raw = sh.v_fresh, sh.q_raw
        k_hi = sb("k_hi", [P, NS, KEYS], F32R)
        k_lo = sb("k_lo", [P, NS, KEYS], F32R)
        q_hi = sb("q_hi", [P, NS, P], F32R)
        q_lo = sb("q_lo", [P, NS, P], F32R)
        seq_f = sb("seq_f", [P, B])
        mask = sb("mask", [P, S + KEYS])
        score = sb("score", [P, 2, KEYS])
        prob = sb("prob", [P, NS, KEYS])
        pn = sb("pn", [P, NS, KEYS])
        top_s = sb("top_s", [P, NS])
        nbias = sb("nbias", [P, NS])
        total = sb("total", [P, NS])
        rtotal = sb("rtotal", [P, NS])
        pT = sb("pT", [P, 2, CACHED])
        pT_fresh = sb("pT_fresh", [2 * S, 2, P])
        o_out = late.o_out
        SP_ = [s.ps(f"scores{i}", [P, 2, 512]) for i in range(2)]
        TPa = s.ps("probsT", [P, 5 * P + 384])
        OP = s.ps("outT", [P, 2, 512])

        seq_cast, mask_zero = sem("seq_cast"), sem("mask_zero")
        pool_passed, dve_passed = sem("pool_passed"), sem("dve_passed")
        vf_in, q_in, o_sent = sh.vf_in, sh.q_in, sh.o_sent
        scale_moved, first_split = sem("scale_moved"), sem("first_split")
        khi_done, klo_done, qhi_done, qlo_done = sem("khi_done"), sem("klo_done"), sem("qhi_done"), sem("qlo_done")
        s_done, mask_done, max_done, bias_done = sem("s_done"), sem("mask_done"), sem("max_done"), sem("bias_done")
        exp_done, rec_done, pn_done = sem("exp_done"), sem("rec_done"), sem("pn_done")
        pt_done, pt_evac, pv_done, o_evac = sem("pt_done"), sem("pt_evac"), sem("pv_done"), sem("o_evac")
        fresh_evac = sem("fresh_evac")

        def run(eng, step, lag, straight_end=False):
            looped = UNITS // TRIP - straight_end
            for j in range(TRIP):
                step(Unit(0, j))
            with eng.Fori(1, looped) as trip:
                for j in range(TRIP):
                    step(Unit(trip * TRIP, j))
            for j in range(UNITS - looped * TRIP + lag):
                step(Unit(looped * TRIP, j))

        def batch(u):
            return (u.base // HK) + u.j // HK

        def places(h):
            return slice(1 - h % 2, 1 - h % 2 + NPG)

        def trips(u, plus=1):
            return (u.base // TRIP) + (u.j // TRIP + plus)

        block = s.ctx.enter_context(nc.Block())

        @block.sync
        def _(sp):
            def load_pages(par, page):
                for n in range(NPP):
                    sp.dma_start(k_raw[:, par, 1 + n, :], kT[bass.ds(page[n], 1)].rearrange("o d c -> d (o c)")).then_inc(k_in[par], 16)

            def store(par, b, done):
                wait(sp, o_evac, done)
                sp.dma_start(o_f[bass.ds(b, 1)].rearrange("o d c -> d (o c)"), o_out[:, par, :]).then_inc(o_sent[par], 16)

            for g in range(2):
                sp.dma_start(sh.wo_raw[:, g, :, :], woT[g].rearrange("r p n -> p r n")).then_inc(sh.wo_in[g], 16)
            for o in range(4):
                sp.wait_ge(sh.kqv_sent[o], 16 * CHUNKS * TILES // 4)
            with sp.Fori(1, UNITS // TRIP) as trip:
                for par in range(2):
                    b, before = trip * 2 + par, trip * TRIP + (par - 1) * HK
                    page = page_numbers(nc, sh.table, b)
                    sp.wait_ge(sh.attn_in, ATTN_IN)
                    wait(sp, qlo_done, before)
                    wait(sp, khi_done, before)
                    wait(sp, klo_done, before)
                    load_fresh(nc, sh, kq_f, par, b)
                    load_pages(par, page)
                    wait(sp, pv_done, before)
                    load_fresh_v(nc, sh, v_f, par, b)
                    store(par, trip * 2 + (par - 2), before)
            for par in range(2):
                store(par, B - 2 + par, UNITS + (par - 1) * HK)

        @block.tensor
        def _(pe):
            def step(u):
                if u.within(UNITS):
                    p2, p4 = u.slot(2), u.slot(NS)
                    wait(pe, klo_done, u.n(1))
                    wait(pe, khi_done, u.n(1))
                    wait(pe, qlo_done, u.n(1))
                    wait(pe, max_done, u.n(-1))
                    for half in range(2):
                        ks = slice(half * HALF, (half + 1) * HALF)
                        out = SP_[p2][:, half, 0:HALF]
                        nc.tensor.matmul(out, q_hi[:, p4, :], k_hi[:, p4, ks], start=True, stop=False)
                        nc.tensor.matmul(out, q_hi[:, p4, :], k_lo[:, p4, ks], start=False, stop=False)
                        mm = nc.tensor.matmul(out, q_lo[:, p4, :], k_hi[:, p4, ks], start=False, stop=True)
                    mm.then_inc(s_done, 1)
                v = u.back(3)
                if v.within(UNITS):
                    wait(pe, pn_done, v.n(1))
                    wait(pe, pt_evac, v.n())
                    at = v.slot(2) * S
                    for c in range(4):
                        tr = nc.tensor.transpose(TPa[:, c * P:(c + 1) * P], pn[:, v.slot(NS), at + c * P:at + (c + 1) * P], ident[:, :])
                    if v.slot(2) == 1:
                        at = (v.slot(NS) - 1) * KEYS + CACHED
                        both = pn[:, :, :].rearrange("p u c -> p (u c)")[:, at:at + 2 * S]
                        tr = nc.tensor.transpose(TPa[0:2 * S, 4 * P:5 * P], both, ident[:, :])
                    tr.then_inc(pt_done, 1)
                w = u.back(4)
                if w.within(UNITS):
                    par, h = (w.j // HK) % 2, w.j % HK
                    hd = slice(h * D, (h + 1) * D)
                    if h == 0:
                        wait(pe, v_in[par], trips(w) * (16 * VCH))
                        wait(pe, vf_in[par], trips(w) * 32)
                    wait(pe, pt_evac, w.n(1))
                    wait(pe, o_evac, w.n(-1))
                    out = OP[:, w.slot(2), 0:P]
                    for c in range(4):
                        nc.tensor.matmul(out, v_raw[:, par, c, hd], pT[:, w.slot(2), c * P:(c + 1) * P], start=(c == 0), stop=False)
                    wait(pe, fresh_evac, w.n(2 - w.slot(2)))
                    rows = slice(w.slot(2) * S, (w.slot(2) + 1) * S)
                    nc.tensor.matmul(out, v_fresh[rows, par, h // 2, :], pT_fresh[rows, (w.j // 2) % 2, :], start=False, stop=True).then_inc(pv_done, 1)

            run(pe, step, 4)

        @block.scalar
        def _(act):
            def step(u):
                v = u.back(3)
                if v.within(UNITS):
                    wait(act, pt_done, v.n(1))
                    if v.slot(2) == 1:
                        wait(act, pv_done, v.n(-3))
                        nc.scalar.copy(pT_fresh[:, (v.j // 2) % 2, :], TPa[0:2 * S, 4 * P:5 * P]).then_inc(fresh_evac, 2)
                    wait(act, pv_done, v.n(-1))
                    nc.scalar.copy(pT[:, v.slot(2), :], TPa[:, 0:4 * P]).then_inc(pt_evac, 1)
                if u.within(UNITS):
                    wait(act, bias_done, u.n(1))
                    wait(act, pn_done, u.n(-3))
                    nc.scalar.activation(prob[:, u.slot(NS), :], score[:, u.slot(2), :], ACT.Exp,
                                         bias=nbias[:, u.slot(NS):u.slot(NS) + 1], scale=q_scale[:, bass.ds(u.n(), 1)],
                                         accum_out=total[:, u.slot(NS):u.slot(NS) + 1]).then_inc(exp_done, 1)
                w = u.back(4)
                if w.within(UNITS):
                    par, h = (w.j // HK) % 2, w.j % HK
                    if h == KEPT:
                        wait(act, o_sent[par], trips(w, 0) * 16)
                    wait(act, pv_done, w.n(1))
                    if w.static() and w.n() == 0:
                        for o in range(4):
                            act.wait_ge(sh.kqv_sent[o], 16 * CHUNKS * TILES // 4)
                    if h < KEPT:
                        dst = sh.o_raw[:, h, bass.ds(batch(w), 1), :].rearrange("p o c -> p (o c)")
                    else:
                        dst = o_out[:, par, (h - KEPT) * P:(h - KEPT + 1) * P]
                    nc.scalar.copy(dst, OP[:, w.slot(2), 0:P]).then_inc(o_evac, 1)

            run(act, step, 4)

        @block.gpsimd
        def _(pool):
            def step(u):
                if u.within(UNITS):
                    par, h, p4 = (u.j // HK) % 2, u.j % HK, u.slot(NS)
                    landed = [(k_in[par], trips(u) * (16 * PLACES))] if h == 0 else []
                    waits(pool, pool_passed, landed + [(s_done, u.n(-3)), (klo_done, u.n(-3))])
                    nc.gpsimd.tensor_scalar(k_hi[:, p4, :].rearrange("p (n c) -> p n c", c=PSIZE),
                                            k_raw[:, par, places(h), h * PSIZE:(h + 1) * PSIZE], 1.0, 1.0, ALU.mult, ALU.mult).then_inc(khi_done, 1)
                x = u.back(GATHER_LAG)
                if x.within(UNITS - HK) and x.j % HK in (0,) + GATHER_AT:
                    h, par = x.j % HK, (x.j // HK + 1) % 2
                    b = batch(x) + 1
                    if h == 0:
                        wait(pool, pv_done, x.n())
                        place_rows(nc, sh, b, par)
                    else:
                        waits(pool, pool_passed, [(sh.row_set, b + 1), (pv_done, x.n(-h))])
                        gather_values(nc, sh, v_c, par, (GATHER_AT.index(h),))
                v = u.back(4)
                if v.within(UNITS):
                    waits(pool, pool_passed, [(rec_done, v.n(1)), (pt_done, v.n(-2))])
                    nc.gpsimd.tensor_scalar(pn[:, v.slot(NS), :], prob[:, v.slot(NS), :], rtotal[:, v.slot(NS):v.slot(NS) + 1], 1.0,
                                            ALU.mult, ALU.mult).then_inc(pn_done, 1)

            run(pool, step, 4, straight_end=True)

        @block.vector
        def _(dve):
            dve.wait_ge(sh.attn_in, ATTN_IN)
            nc.vector.tensor_copy(seq_f[:, :], sh.seq_i[:, :]).then_inc(seq_cast, 1)
            nc.vector.memset(mask[:, 0:S], 0.0)
            nc.vector.memset(mask[:, S + CACHED:], 0.0).then_inc(mask_zero, 1)
            dve.wait_ge(seq_cast, 1)
            dve.wait_ge(mask_zero, 1)

            def move_scales():
                qs = q_scale[:, :].rearrange("p (t b k) -> p t b k", b=BT, k=HK)
                qr = sh.q_rs[:, :, :].rearrange("p t (k r) -> p t k r", r=R)
                for bl in range(BT):
                    for r in range(R):
                        last = nc.vector.tensor_scalar(qs[r * S:(r + 1) * S, :, bl, :], qr[bl * S:(bl + 1) * S, :, :, r], SCALE, None, ALU.mult)
                last.then_inc(scale_moved, 1)
                dve.wait_ge(scale_moved, 1)
                nc.vector.tensor_scalar(sh.q_nscale[:, :], q_scale[:, :], -1.0, None, ALU.mult).then_inc(scale_moved, 1)
                dve.wait_ge(scale_moved, 2)

            def split_first_weight():
                dve.wait_ge(sh.wo_in[0], 16)
                nc.vector.tensor_copy(late.w_hi[:, :], sh.wo_raw[:, 0, 0, :]).then_inc(first_split, 1)
                dve.wait_ge(first_split, 1)
                nc.vector.tensor_tensor(late.w_lo[:, :], sh.wo_raw[:, 0, 0, :], late.w_hi[:, :].bitcast(F32), ALU.subtract).then_inc(first_split, 1)

            def step(u):
                if u.static() and u.n() == 1:
                    move_scales()
                if u.static() and u.n() == UNITS + 2:
                    split_first_weight()
                if u.within(UNITS):
                    par, h, p4 = (u.j // HK) % 2, u.j % HK, u.slot(NS)
                    if h == 0:
                        wait(dve, q_in[par], trips(u) * 16)
                    wait(dve, s_done, u.n(-3))
                    nc.vector.tensor_copy(q_hi[:, p4, :], q_raw[:, par, h * P:(h + 1) * P]).then_inc(qhi_done, 1)
                    wait(dve, khi_done, u.n(1))
                    nc.vector.tensor_tensor(k_lo[:, p4, :].rearrange("p (n c) -> p n c", c=PSIZE),
                                            k_raw[:, par, places(h), h * PSIZE:(h + 1) * PSIZE],
                                            k_hi[:, p4, :].bitcast(F32).rearrange("p (n c) -> p n c", c=PSIZE), ALU.subtract).then_inc(klo_done, 1)
                    wait(dve, qhi_done, u.n(1))
                    nc.vector.tensor_tensor(q_lo[:, p4, :], q_raw[:, par, h * P:(h + 1) * P], q_hi[:, p4, :].bitcast(F32), ALU.subtract).then_inc(qlo_done, 1)
                v = u.back(2)
                if v.within(UNITS):
                    par, h, p4 = (v.j // HK) % 2, v.j % HK, v.slot(NS)
                    if h == 0:
                        wait(dve, max_done, v.n())
                        nc.vector.tensor_scalar(mask[:, S:S + CACHED], sh.key[:, :], seq_f[:, bass.ds(batch(v), 1)], MASKED,
                                                ALU.is_ge, ALU.mult).then_inc(mask_done, 1)
                    masked = [(mask_done, batch(v) + 1)] if h == 0 else []
                    waits(dve, dve_passed, masked + [(s_done, v.n(1)), (exp_done, v.n(-1))])
                    nc.vector.tensor_tensor_reduce(score[:, v.slot(2), :].rearrange("p (a c) -> p a c", a=2), SP_[v.slot(2)][:, :, 0:HALF],
                                                   mask[:, places(h).start * S:places(h).start * S + KEYS].rearrange("p (a c) -> p a c", a=2), 1.0, -3e38, ALU.add, ALU.max,
                                                   accum_out=top_s[:, p4:p4 + 1]).then_inc(max_done, 1)
                w = u.back(3)
                if w.within(UNITS):
                    p4 = w.slot(NS)
                    wait(dve, exp_done, w.n(1))
                    wait(dve, pn_done, w.n(-3))
                    nc.vector.reciprocal(rtotal[:, p4:p4 + 1], total[:, p4:p4 + 1]).then_inc(rec_done, 1)
                if v.within(UNITS):
                    p4 = v.slot(NS)
                    wait(dve, max_done, v.n(1))
                    nc.vector.tensor_tensor(nbias[:, p4:p4 + 1], top_s[:, p4:p4 + 1], sh.q_nscale[:, bass.ds(v.n(), 1)], ALU.mult).then_inc(bias_done, 1)

            run(dve, step, 3)
            dve.wait_ge(o_evac, UNITS - HK + 1)
            o_src = sh.o_raw[:, 0, :, 0:S]
            o_hi, o_lo = (t.rearrange("p (b s) -> p b s", s=S) for t in (late.o_hi, late.o_lo))
            nc.vector.tensor_copy(o_hi, o_src).then_inc(first_split, 1)
            dve.wait_ge(first_split, 3)
            nc.vector.tensor_tensor(o_lo, o_src, o_hi.bitcast(F32), ALU.subtract)


def finish(nc, sh, late, x_tok, woT, cond, mix, o_f, out):
    s = Scope(nc)
    sb, sem = s.sb, s.sem
    with s.ctx:
        o_raw, w_raw, o_in, w_in = sh.o_raw, sh.wo_raw, sh.o_in, sh.wo_in
        o_hi = [late.o_hi, sb("o_hi_odd", [P, TOK], F32R)]
        o_lo = [late.o_lo, sb("o_lo_odd", [P, TOK], F32R)]
        w_hi = [late.w_hi, sb("wo_hi_odd", [P, HID], F32R)]
        w_lo = [late.w_lo, sb("wo_lo_odd", [P, HID], F32R)]
        x_sb = sb("x_sb", [P, TILES, HID])
        y_sb = sb("y_sb", [P, TILES, HID])
        cond_sb = sb("cond_sb", [1, B], I32)
        blocks = sb("blocks", [P, TILES, P])
        Y = [s.ps(f"Y{i}", [P, HID]) for i in range(TILES)]
        x_in, cond_in, zeroed, mix_in = sem("x_tok_in"), sem("cond_in"), sem("zeroed"), sem("mix_in")
        ohi_done, whi_done, parts_done, tile_done = sem("ohi_done"), sem("whi_done"), sem("parts_done"), sem("tile_done")
        res_done, mix_done, y_done, stored = sem("res_done"), sem("mixed"), sem("y_done"), sem("stored")

        def run(eng, step):
            for j in range(2 * R):
                step(Unit(0, j))
            with eng.Fori(1, HK // 2) as trip:
                for j in range(2 * R):
                    step(Unit(trip * (2 * R), j))

        block = s.ctx.enter_context(nc.Block())

        @block.sync
        def _(sp):
            def load(par, g, before):
                wait(sp, parts_done, before - 1)
                sp.dma_start(o_raw[:, par, :, :], o_f[:, :, bass.ds((g - KEPT) * P, P)].rearrange("b d c -> d b c")).then_inc(o_in[par], 16)
                sp.dma_start(w_raw[:, par, :, :], woT[bass.ds(g, 1)].rearrange("o r p n -> p (o r) n")).then_inc(w_in[par], 16)
            sp.dma_start(x_sb[:, :, :], x_tok.rearrange("(t p) n -> p t n", p=P)).then_inc(x_in, 16)
            for par in range(2):
                sp.wait_ge(sh.o_sent[par], 16 * B // 2)
            with sp.Fori(1, HK // 2) as trip:
                for par in range(2):
                    load(par, trip * 2 + par, trip * (2 * R) + (par - 1) * R)
            o_tiles = out.rearrange("(t p) n -> t p n", p=P)
            for t in range(TILES):
                sp.wait_ge(y_done, t + 1)
                sp.dma_start(o_tiles[t], y_sb[:, t, :]).then_inc(stored, 16)
            sp.wait_ge(stored, 16 * TILES)

        @block.scalar
        def _(act):
            act.dma_start(cond_sb[:, :], cond).then_inc(cond_in, 16)
            act.wait_ge(cond_in, 16)
            act.wait_ge(zeroed, 1)
            for b in range(B):
                c = act.value_load(cond_sb[0:1, b:b + 1], min_val=0, max_val=15)
                q = (b % BT) * S
                act.dma_start(blocks[q:q + S, b // BT, q:q + S], mix[bass.ds(c, 1)].rearrange("o c d -> c (o d)")).then_inc(mix_in, 16)

        @block.gpsimd
        def _(pool):
            nc.gpsimd.memset(blocks[:, :, :], 0.0).then_inc(zeroed, 1)

        @block.vector
        def _(dve):
            def step(u):
                if u.static() and u.n() == 0:
                    return
                par, r, p2 = (u.j // R) % 2, u.j % R, u.slot(2)
                if r == 0:
                    wait(dve, o_in[par], (u.base // (2 * R)) * 16)
                    wait(dve, w_in[par], (u.base // (2 * R)) * 16 + 16)
                wait(dve, tile_done, u.n(-1) * TILES)
                src = o_raw[:, par, :, r * S:(r + 1) * S]
                hi, lo = (t[p2].rearrange("p (b s) -> p b s", s=S) for t in (o_hi, o_lo))
                nc.vector.tensor_copy(w_hi[p2][:, :], w_raw[:, par, r, :]).then_inc(whi_done, 1)
                nc.vector.tensor_copy(hi, src).then_inc(ohi_done, 1)
                wait(dve, whi_done, u.n())
                nc.vector.tensor_tensor(w_lo[p2][:, :], w_raw[:, par, r, :], w_hi[p2][:, :].bitcast(F32), ALU.subtract)
                wait(dve, ohi_done, u.n())
                nc.vector.tensor_tensor(lo, src, hi.bitcast(F32), ALU.subtract).then_inc(parts_done, 1)

            run(dve, step)
            dve.wait_ge(x_in, 16)
            for t in range(TILES + 2):
                if t < TILES:
                    dve.wait_ge(tile_done, (HQ - 1) * TILES + t + 1)
                    nc.vector.tensor_tensor(x_sb[:, t, :], x_sb[:, t, :], Y[t][:, :], ALU.add).then_inc(res_done, 1)
                if t >= 2:
                    dve.wait_ge(mix_done, t - 1)
                    nc.vector.tensor_tensor(y_sb[:, t - 2, :], x_sb[:, t - 2, :], Y[t - 2][:, :], ALU.add).then_inc(y_done, 1)

        @block.tensor
        def _(pe):
            def step(u):
                p2 = u.slot(2)
                first = u.static() and u.n() == 0
                wait(pe, parts_done, u.n())
                for t in range(TILES):
                    cols = slice(t * P, (t + 1) * P)
                    nc.tensor.matmul(Y[t][:, :], o_hi[p2][:, cols], w_hi[p2][:, :], start=first, stop=False, skip_group_check=True)
                    nc.tensor.matmul(Y[t][:, :], o_hi[p2][:, cols], w_lo[p2][:, :], start=False, stop=False, skip_group_check=True)
                    nc.tensor.matmul(Y[t][:, :], o_lo[p2][:, cols], w_hi[p2][:, :], start=False, stop=True, skip_group_check=True).then_inc(tile_done, 1)

            run(pe, step)
            pe.wait_ge(mix_in, 16 * B)
            for t in range(TILES):
                pe.wait_ge(res_done, t + 1)
                nc.tensor.matmul(Y[t][:, :], blocks[:, t, :], x_sb[:, t, :], start=True, stop=True).then_inc(mix_done, 1)


def program(nc, xT, x_tok, w_all, woT, seq, seq_tile, pages, page_of_chunk, cond, q_w, k_w, kT, v_c, mix, inv_freq, sidx, iota, eye, out):
    kq_f = nc.dram_tensor("kq_fresh", [B, D, HK * S + HK * P], F32).ap()
    v_f = nc.dram_tensor("v_fresh_all", [B, S, HK * D], F32).ap()
    o_f = nc.dram_tensor("heads_out", [B, D, (HK - KEPT) * P], F32).ap()
    sh = Shared(nc)
    with sh.ctx:
        project(nc, sh, xT, w_all, seq_tile, seq, inv_freq, sidx, q_w, k_w, pages, page_of_chunk, kT, v_c, iota, eye, kq_f, v_f.rearrange("b s c -> (b s) c"))
        late = Late(nc)
        with late.ctx:
            attend(nc, sh, late, kT, v_c, kq_f, v_f, o_f, woT)
            finish(nc, sh, late, x_tok, woT, cond, mix, o_f, out)


def kernel(**inputs):
    import concourse.bacc as _bacc
    from concourse.bass_utils import run_bass_kernel_spmd as _run

    a = {k: np.asarray(v) for k, v in inputs.items()}
    cont = np.ascontiguousarray
    x = a["x"].reshape(TOK, HID)
    w_all = np.concatenate([a["L0_cond_Wv"], a["L0_cond_Wk"], a["L0_cond_Wq"]], axis=0)
    half = np.arange(0, D, 2, dtype=np.float32) / np.float32(D)
    arrays = {
        "xT": cont(x.T.reshape(KC, P, TOK).transpose(1, 0, 2)),
        "x_tok": cont(x),
        "w_all": cont(w_all.reshape(CHUNKS, NC_, KC, P).transpose(0, 3, 2, 1)),
        "woT": cont(a["L0_cond_Wo"].T.reshape(HK, R, P, HID)),
        "seq": cont(a["itok_B_207_1644"]),
        "seq_tile": cont(a["itok_B_207_1644"].reshape(TILES, BT).T.reshape(-1)),
        "pages": cont(a["itok_Bx16_0_63"].reshape(1, B * NPP)),
        "page_of_chunk": cont(a["itok_Bx16_0_63"].reshape(B * VCH, BT).T),
        "cond": cont(a["itok_B_0_15"].reshape(1, B)),
        "q_w": cont(a["L0_cond_q_norm_w"]),
        "k_w": cont(a["L0_cond_k_norm_w"]),
        "kT": cont(a["L0_cond_k_cache"].transpose(0, 3, 2, 1).reshape(PAGES, D, HK * PSIZE)),
        "v_c": cont(a["L0_cond_v_cache"].reshape(PAGES * PSIZE, HK * D)),
        "mix": cont(a["L1_cond_weights"]),
        "inv_freq": (np.float32(1) / (10000.0 ** half.astype(np.float64)).astype(np.float32)).astype(np.float32),
        "sidx": (np.arange(P) % S).astype(np.float32).reshape(P, 1),
        "iota": np.arange(CACHED).astype(np.float32),
        "eye": np.eye(P, dtype=np.float32),
    }
    nc = _bacc.Bacc("TRN2", target_bir_lowering=False, num_devices=1)
    args = [nc.dram_tensor(f"in_{k}", v.shape, mybir.dt.from_np(v.dtype), kind="ExternalInput").ap() for k, v in arrays.items()]
    out = nc.dram_tensor("out_y", [TOK, HID], F32, kind="ExternalOutput").ap()
    program(nc, *args, out)
    r = _run(nc, [{f"in_{k}": v for k, v in arrays.items()}], core_ids=[0])
    return r.results[0]["out_y"].reshape(B, S, HID)
```
